# Optimizing a Trainium2 kernel written in Bass

```python
import numpy as np
import jax
import jax.numpy as jnp

def _softmax(x, axis=-1):
    return jax.nn.softmax(x, axis=axis)

def _gelu(x):
    return jax.nn.gelu(x, approximate=True)

def _silu(x):
    return jax.nn.silu(x)

def _sigmoid(x):
    return jax.nn.sigmoid(x)

def _layernorm(x, axis=-1, eps=1e-05):
    m = jnp.mean(x, axis=axis, keepdims=True)
    v = jnp.var(x, axis=axis, keepdims=True)
    return (x - m) / jnp.sqrt(v + eps)

def _scatter_add(tgt, idx, src, axis=0):
    return tgt.at[idx].add(src)

def _segment_sum(src, seg, n):
    return jax.ops.segment_sum(src, seg, n)
kernel_name = 'mk_gnn_ffn_d4_gnn_r32_7debb0'

def setup_inputs(seed: int=0):
    np.random.seed(seed)
    _w = jnp.asarray

    def _rec_inputs():
        import jax
        import jax.numpy as jnp
        _gk = jax.random.key(seed)
        x = -0.000364 + 1 * jax.random.normal(jax.random.fold_in(_gk, 1), (625, 768), jnp.float32)
        src = jax.random.randint(jax.random.fold_in(_gk, 2), (10000,), 0, 625, jnp.int32)
        dst = jax.random.randint(jax.random.fold_in(_gk, 3), (10000,), 0, 625, jnp.int32)
        _o = jnp.argsort(dst, stable=True)
        src = src[_o]
        dst = dst[_o]
        edge_type_3 = jax.random.randint(jax.random.fold_in(_gk, 12), (10000,), 0, 3, jnp.int32)
        return (x, src, dst, edge_type_3)
    x, src, dst, edge_type_3 = _rec_inputs()

    def _L0_gnn_setup():
        import jax, jax.numpy as jnp
        import numpy as np
        N = 625
        E = 10000
        D = 768
        H = 4
        C = D // H
        NEG_SLOPE = 0.2

        def gat_layer(x, src, dst, W, a_src, a_dst, b):
            h = (x @ W).reshape(-1, H, C)
            as_ = jnp.sum(h * a_src, axis=-1)
            ad_ = jnp.sum(h * a_dst, axis=-1)
            e = jax.nn.leaky_relu(as_[src] + ad_[dst], NEG_SLOPE)
            m = jax.ops.segment_max(e, dst, num_segments=N)
            e = jnp.exp(e - m[dst])
            s = jax.ops.segment_sum(e, dst, num_segments=N)
            alpha = e / s[dst]
            msg = h[src] * alpha[:, :, None]
            out = jax.ops.segment_sum(msg, dst, num_segments=N)
            return out.reshape(-1, H * C) + b
        key = jax.random.key(seed)
        ks = jax.random.split(key, 10)
        x = jax.random.normal(ks[0], (N, D), dtype=jnp.float32)
        edge_index = jax.random.randint(ks[1], (2, E), 0, N, dtype=jnp.int64)
        sc = 0.05
        W1 = jax.random.normal(ks[2], (D, H * C), dtype=jnp.float32) * sc
        a_src1 = jax.random.normal(ks[3], (H, C), dtype=jnp.float32) * sc
        a_dst1 = jax.random.normal(ks[4], (H, C), dtype=jnp.float32) * sc
        b1 = jnp.zeros((H * C,), dtype=jnp.float32)
        W2 = jax.random.normal(ks[5], (H * C, H * C), dtype=jnp.float32) * sc
        a_src2 = jax.random.normal(ks[6], (H, C), dtype=jnp.float32) * sc
        a_dst2 = jax.random.normal(ks[7], (H, C), dtype=jnp.float32) * sc
        b2 = jnp.zeros((H * C,), dtype=jnp.float32)
        return {'x': x, 'edge_index': edge_index, 'W1': W1, 'a_src1': a_src1, 'a_dst1': a_dst1, 'b1': b1, 'W2': W2, 'a_src2': a_src2, 'a_dst2': a_dst2, 'b2': b2}
    _L0_gnn_all = _L0_gnn_setup()
    _L0_gnn_in = {k: v for k, v in _L0_gnn_all.items() if k in ('W1', 'a_src1', 'a_dst1', 'b1', 'W2', 'a_src2', 'a_dst2', 'b2')}
    del _L0_gnn_all

    def _L0_ffn_setup():
        import jax, jax.numpy as jnp
        import numpy as np

        def _fq(x, scale, qmin, qmax):
            q = jnp.clip(jnp.round(x / scale), qmin, qmax) * scale
            return x + jax.lax.stop_gradient(q - x)

        def _quant_weight(W):
            scale = jnp.max(jnp.abs(W)) / 127.0
            return _fq(W, scale, -127.0, 127.0)
        key = jax.random.key(seed)
        ks = jax.random.split(key, 5)
        B, S, D, H = (64, 196, 768, 96)
        x = jax.random.normal(ks[0], (B, S, D), dtype=jnp.float32)
        W1 = jax.random.normal(ks[1], (H, D), dtype=jnp.float32) * D ** (-0.5)
        b1 = jax.random.normal(ks[2], (H,), dtype=jnp.float32) * 0.01
        W2 = jax.random.normal(ks[3], (D, H), dtype=jnp.float32) * H ** (-0.5)
        b2 = jax.random.normal(ks[4], (D,), dtype=jnp.float32) * 0.01
        s_gelu = jnp.float32(0.05)
        s_out = jnp.float32(0.02)
        return {'x': x, 'W1': W1, 'b1': b1, 'W2': W2, 'b2': b2, 's_gelu': s_gelu, 's_out': s_out}
    _L0_ffn_all = _L0_ffn_setup()
    _L0_ffn_in = {k: v for k, v in _L0_ffn_all.items() if k in ('W1', 'b1', 'W2', 'b2', 's_gelu', 's_out')}
    del _L0_ffn_all

    def _L1_gnn_setup():
        import jax, jax.numpy as jnp
        import numpy as np
        N_NODES = 10000
        N_EDGES = 3125
        DIM = 768
        NEG_SLOPE = 0.2

        def gat_conv(x, src, dst, W, att_src, att_dst, bias, num_nodes):
            h = x @ W
            a_s = h @ att_src
            a_d = h @ att_dst
            e = jax.nn.leaky_relu(a_s[src] + a_d[dst], NEG_SLOPE)
            m = jax.ops.segment_max(e, dst, num_segments=num_nodes)
            e = jnp.exp(e - m[dst])
            denom = jax.ops.segment_sum(e, dst, num_segments=num_nodes)
            alpha = e / denom[dst]
            msg = alpha[:, None] * h[src]
            out = jax.ops.segment_sum(msg, dst, num_segments=num_nodes)
            return out + bias
        key = jax.random.key(seed)
        ks = jax.random.split(key, 12)
        s = 1.0 / np.sqrt(DIM)
        inp = {'x': jax.random.normal(ks[0], (N_NODES, DIM), dtype=jnp.float32), 'edge_index': jax.random.randint(ks[1], (2, N_EDGES), 0, N_NODES, dtype=jnp.int64), 'W1': jax.random.normal(ks[2], (DIM, DIM), dtype=jnp.float32) * s, 'att_src1': jax.random.normal(ks[3], (DIM,), dtype=jnp.float32) * s, 'att_dst1': jax.random.normal(ks[4], (DIM,), dtype=jnp.float32) * s, 'b1': jnp.zeros((DIM,), dtype=jnp.float32), 'W2': jax.random.normal(ks[5], (DIM, DIM), dtype=jnp.float32) * s, 'att_src2': jax.random.normal(ks[6], (DIM,), dtype=jnp.float32) * s, 'att_dst2': jax.random.normal(ks[7], (DIM,), dtype=jnp.float32) * s, 'b2': jnp.zeros((DIM,), dtype=jnp.float32)}
        return inp
    _L1_gnn_all = _L1_gnn_setup()
    _L1_gnn_in = {k: v for k, v in _L1_gnn_all.items() if k in ('W1', 'att_src1', 'att_dst1', 'b1', 'W2', 'att_src2', 'att_dst2', 'b2')}
    del _L1_gnn_all

    def _L1_ffn_setup():
        import jax, jax.numpy as jnp
        import numpy as np
        B, S, H, D, E = (4, 64, 768, 1024, 8)
        TOP_K = 2
        EPS = 1e-08
        LN_EPS = 1e-05

        def _gelu(t):
            return jax.nn.gelu(t, approximate=False)

        def _layer_norm(t, gamma, beta):
            mu = jnp.mean(t, axis=-1, keepdims=True)
            var = jnp.mean(jnp.square(t - mu), axis=-1, keepdims=True)
            return (t - mu) * jax.lax.rsqrt(var + LN_EPS) * gamma + beta
        key = jax.random.key(seed)
        ks = jax.random.split(key, 8)
        x = jax.random.normal(ks[0], (B, S, H), dtype=jnp.float32)
        w1 = jax.random.normal(ks[1], (H, H // 2), dtype=jnp.float32) * 0.02
        b1 = jnp.zeros((H // 2,), dtype=jnp.float32)
        w2 = jax.random.normal(ks[2], (H // 2, E), dtype=jnp.float32) * 0.02
        b2 = jnp.zeros((E,), dtype=jnp.float32)
        a_dn = float(np.sqrt(6.0 / (H + D)))
        a_up = float(np.sqrt(6.0 / (D + H)))
        down_w = jax.random.uniform(ks[3], (E, H, D), dtype=jnp.float32, minval=-a_dn, maxval=a_dn)
        down_b = jnp.zeros((E, D), dtype=jnp.float32)
        up_w = jax.random.uniform(ks[4], (E, D, H), dtype=jnp.float32, minval=-a_up, maxval=a_up)
        gamma = jnp.ones((H,), dtype=jnp.float32)
        beta = jnp.zeros((H,), dtype=jnp.float32)
        return {'x': x, 'w1': w1, 'b1': b1, 'w2': w2, 'b2': b2, 'down_w': down_w, 'down_b': down_b, 'up_w': up_w, 'gamma': gamma, 'beta': beta}
    _L1_ffn_all = _L1_ffn_setup()
    _L1_ffn_in = {k: v for k, v in _L1_ffn_all.items() if k in ('w1', 'b1', 'w2', 'b2', 'down_w', 'down_b', 'up_w', 'gamma', 'beta')}
    del _L1_ffn_all

    def _L2_gnn_setup():
        import jax, jax.numpy as jnp
        import numpy as np
        N_NODES = 10000
        N_EDGES = 3125
        DIM = 768
        key = jax.random.key(seed)
        k1, k2, k3, k4 = jax.random.split(key, 4)
        x = jax.random.normal(k1, (N_NODES, DIM), dtype=jnp.float32)
        edge_index = jax.random.randint(k2, (2, N_EDGES), 0, N_NODES, dtype=jnp.int32)
        W = jax.random.normal(k3, (DIM, DIM), dtype=jnp.float32) / np.sqrt(DIM)
        b = jnp.zeros((DIM,), dtype=jnp.float32)
        return {'x': x, 'edge_index': edge_index, 'W': W, 'b': b}
    _L2_gnn_all = _L2_gnn_setup()
    _L2_gnn_in = {k: v for k, v in _L2_gnn_all.items() if k in ('W', 'b')}
    del _L2_gnn_all

    def _L2_ffn_setup():
        import jax, jax.numpy as jnp
        import numpy as np
        E, C, F, K = (8, 768, 96, 2)
        key = jax.random.key(seed)
        k0, k1, k2, k3 = jax.random.split(key, 4)
        B, T = (8, 64)
        return {'x': jax.random.normal(k0, (B, T, C), jnp.float32), 'router_w': jax.random.normal(k1, (E, C), jnp.float32) * 0.02, 'w1': jax.random.normal(k2, (E, C, F), jnp.float32) * 0.02, 'b1': jnp.zeros((E, F), jnp.float32), 'w2': jax.random.normal(k3, (E, F, C), jnp.float32) * 0.02, 'b2': jnp.zeros((E, C), jnp.float32)}
    _L2_ffn_all = _L2_ffn_setup()
    _L2_ffn_in = {k: v for k, v in _L2_ffn_all.items() if k in ('router_w', 'w1', 'b1', 'w2', 'b2')}
    del _L2_ffn_all

    def _L3_gnn_setup():
        import jax, jax.numpy as jnp
        import numpy as np
        NEG_SLOPE = 0.2
        EPS = 1e-16
        N_NODES = 1024
        N_EDGES = 5000
        DIM = 768
        HEADS1 = 4
        OUT1 = DIM // HEADS1
        HEADS2 = 1
        OUT2 = DIM
        N_REL = 3

        def rgat_conv(x, W, q, k, b, src, dst, etype, heads, out_ch, n_nodes):
            xr = jnp.einsum('nd,rdf->rnf', x, W)
            oi = xr[etype, dst]
            oj = xr[etype, src]
            qi = oi @ q
            kj = oj @ k
            alpha = jax.nn.leaky_relu(qi + kj, NEG_SLOPE)
            m = jax.ops.segment_max(alpha, dst, num_segments=n_nodes)
            e = jnp.exp(alpha - m[dst])
            z = jax.ops.segment_sum(e, dst, num_segments=n_nodes)
            a = e / (z[dst] + EPS)
            msg = (a[:, :, None] * oj.reshape(-1, heads, out_ch)).reshape(-1, heads * out_ch)
            out = jax.ops.segment_sum(msg, dst, num_segments=n_nodes)
            return out + b
        key = jax.random.key(seed)
        ks = jax.random.split(key, 12)
        s = 0.02
        return {'x': jax.random.normal(ks[0], (N_NODES, DIM), dtype=jnp.float32), 'edge_index': jax.random.randint(ks[1], (2, N_EDGES), 0, N_NODES, dtype=jnp.int64), 'edge_type': jax.random.randint(ks[2], (N_EDGES,), 0, N_REL, dtype=jnp.int64), 'W1': jax.random.normal(ks[3], (N_REL, DIM, HEADS1 * OUT1), dtype=jnp.float32) * s, 'q1': jax.random.normal(ks[4], (HEADS1 * OUT1, HEADS1), dtype=jnp.float32) * s, 'k1': jax.random.normal(ks[5], (HEADS1 * OUT1, HEADS1), dtype=jnp.float32) * s, 'b1': jnp.zeros((HEADS1 * OUT1,), dtype=jnp.float32), 'W2': jax.random.normal(ks[6], (N_REL, DIM, HEADS2 * OUT2), dtype=jnp.float32) * s, 'q2': jax.random.normal(ks[7], (HEADS2 * OUT2, HEADS2), dtype=jnp.float32) * s, 'k2': jax.random.normal(ks[8], (HEADS2 * OUT2, HEADS2), dtype=jnp.float32) * s, 'b2': jnp.zeros((HEADS2 * OUT2,), dtype=jnp.float32)}
    _L3_gnn_all = _L3_gnn_setup()
    _L3_gnn_in = {k: v for k, v in _L3_gnn_all.items() if k in ('W1', 'q1', 'k1', 'b1', 'W2', 'q2', 'k2', 'b2')}
    del _L3_gnn_all

    def _L3_ffn_setup():
        import jax, jax.numpy as jnp
        import numpy as np
        EPS_NORM = 1e-06
        EPS_Q = 1e-05

        def rmsnorm(x, g):
            return x * jax.lax.rsqrt(jnp.mean(x * x, axis=-1, keepdims=True) + EPS_NORM) * g

        def activation_quant(x):
            scale = 127.0 / jnp.maximum(jnp.max(jnp.abs(x), axis=-1, keepdims=True), EPS_Q)
            return jnp.clip(jnp.round(x * scale), -128, 127) / scale

        def weight_quant(w):
            scale = 1.0 / jnp.maximum(jnp.mean(jnp.abs(w)), EPS_Q)
            return jnp.clip(jnp.round(w * scale), -1, 1) / scale

        def bitlinear(x, w, g):
            x_norm = rmsnorm(x, g)
            x_q = x_norm + jax.lax.stop_gradient(activation_quant(x_norm) - x_norm)
            w_q = w + jax.lax.stop_gradient(weight_quant(w) - w)
            return jnp.einsum('bsd,od->bso', x_q, w_q)
        key = jax.random.key(seed)
        k1, k2, k3 = jax.random.split(key, 3)
        B, S, D, H = (8, 128, 768, 64)
        x = jax.random.normal(k1, (B, S, D), dtype=jnp.float32)
        w_in = jax.random.normal(k2, (2 * H, D), dtype=jnp.float32) * 0.002
        w_out = jax.random.normal(k3, (D, H), dtype=jnp.float32) * 0.002
        g_in = jnp.ones((D,), dtype=jnp.float32)
        g_out = jnp.ones((H,), dtype=jnp.float32)
        return {'x': x, 'w_in': w_in, 'g_in': g_in, 'w_out': w_out, 'g_out': g_out}
    _L3_ffn_all = _L3_ffn_setup()
    _L3_ffn_in = {k: v for k, v in _L3_ffn_all.items() if k in ('w_in', 'g_in', 'w_out', 'g_out')}
    del _L3_ffn_all
    return {'x': x, 'src': src, 'dst': dst, 'edge_type_3': edge_type_3, 'L0_gnn_W1': _L0_gnn_in['W1'], 'L0_gnn_a_src1': _L0_gnn_in['a_src1'], 'L0_gnn_a_dst1': _L0_gnn_in['a_dst1'], 'L0_gnn_b1': _L0_gnn_in['b1'], 'L0_gnn_W2': _L0_gnn_in['W2'], 'L0_gnn_a_src2': _L0_gnn_in['a_src2'], 'L0_gnn_a_dst2': _L0_gnn_in['a_dst2'], 'L0_gnn_b2': _L0_gnn_in['b2'], 'L0_ffn_W1': _L0_ffn_in['W1'], 'L0_ffn_b1': _L0_ffn_in['b1'], 'L0_ffn_W2': _L0_ffn_in['W2'], 'L0_ffn_b2': _L0_ffn_in['b2'], 'L0_ffn_s_gelu': _L0_ffn_in['s_gelu'], 'L0_ffn_s_out': _L0_ffn_in['s_out'], 'L1_gnn_W1': _L1_gnn_in['W1'], 'L1_gnn_att_src1': _L1_gnn_in['att_src1'], 'L1_gnn_att_dst1': _L1_gnn_in['att_dst1'], 'L1_gnn_b1': _L1_gnn_in['b1'], 'L1_gnn_W2': _L1_gnn_in['W2'], 'L1_gnn_att_src2': _L1_gnn_in['att_src2'], 'L1_gnn_att_dst2': _L1_gnn_in['att_dst2'], 'L1_gnn_b2': _L1_gnn_in['b2'], 'L1_ffn_w1': _L1_ffn_in['w1'], 'L1_ffn_b1': _L1_ffn_in['b1'], 'L1_ffn_w2': _L1_ffn_in['w2'], 'L1_ffn_b2': _L1_ffn_in['b2'], 'L1_ffn_down_w': _L1_ffn_in['down_w'], 'L1_ffn_down_b': _L1_ffn_in['down_b'], 'L1_ffn_up_w': _L1_ffn_in['up_w'], 'L1_ffn_gamma': _L1_ffn_in['gamma'], 'L1_ffn_beta': _L1_ffn_in['beta'], 'L2_gnn_W': _L2_gnn_in['W'], 'L2_gnn_b': _L2_gnn_in['b'], 'L2_ffn_router_w': _L2_ffn_in['router_w'], 'L2_ffn_w1': _L2_ffn_in['w1'], 'L2_ffn_b1': _L2_ffn_in['b1'], 'L2_ffn_w2': _L2_ffn_in['w2'], 'L2_ffn_b2': _L2_ffn_in['b2'], 'L3_gnn_W1': _L3_gnn_in['W1'], 'L3_gnn_q1': _L3_gnn_in['q1'], 'L3_gnn_k1': _L3_gnn_in['k1'], 'L3_gnn_b1': _L3_gnn_in['b1'], 'L3_gnn_W2': _L3_gnn_in['W2'], 'L3_gnn_q2': _L3_gnn_in['q2'], 'L3_gnn_k2': _L3_gnn_in['k2'], 'L3_gnn_b2': _L3_gnn_in['b2'], 'L3_ffn_w_in': _L3_ffn_in['w_in'], 'L3_ffn_g_in': _L3_ffn_in['g_in'], 'L3_ffn_w_out': _L3_ffn_in['w_out'], 'L3_ffn_g_out': _L3_ffn_in['g_out']}

def reference(x, src, dst, edge_type_3, L0_gnn_W1, L0_gnn_a_src1, L0_gnn_a_dst1, L0_gnn_b1, L0_gnn_W2, L0_gnn_a_src2, L0_gnn_a_dst2, L0_gnn_b2, L0_ffn_W1, L0_ffn_b1, L0_ffn_W2, L0_ffn_b2, L0_ffn_s_gelu, L0_ffn_s_out, L1_gnn_W1, L1_gnn_att_src1, L1_gnn_att_dst1, L1_gnn_b1, L1_gnn_W2, L1_gnn_att_src2, L1_gnn_att_dst2, L1_gnn_b2, L1_ffn_w1, L1_ffn_b1, L1_ffn_w2, L1_ffn_b2, L1_ffn_down_w, L1_ffn_down_b, L1_ffn_up_w, L1_ffn_gamma, L1_ffn_beta, L2_gnn_W, L2_gnn_b, L2_ffn_router_w, L2_ffn_w1, L2_ffn_b1, L2_ffn_w2, L2_ffn_b2, L3_gnn_W1, L3_gnn_q1, L3_gnn_k1, L3_gnn_b1, L3_gnn_W2, L3_gnn_q2, L3_gnn_k2, L3_gnn_b2, L3_ffn_w_in, L3_ffn_g_in, L3_ffn_w_out, L3_ffn_g_out):
    import jax
    import jax.numpy as jnp

    def _L0_gnn_ref(x, edge_index, W1, a_src1, a_dst1, b1, W2, a_src2, a_dst2, b2):
        import jax, jax.numpy as jnp
        import numpy as np
        N = 625
        E = 10000
        D = 768
        H = 4
        C = D // H
        NEG_SLOPE = 0.2

        def gat_layer(x, src, dst, W, a_src, a_dst, b):
            h = (x @ W).reshape(-1, H, C)
            as_ = jnp.sum(h * a_src, axis=-1)
            ad_ = jnp.sum(h * a_dst, axis=-1)
            e = jax.nn.leaky_relu(as_[src] + ad_[dst], NEG_SLOPE)
            m = jax.ops.segment_max(e, dst, num_segments=N)
            e = jnp.exp(e - m[dst])
            s = jax.ops.segment_sum(e, dst, num_segments=N)
            alpha = e / s[dst]
            msg = h[src] * alpha[:, :, None]
            out = jax.ops.segment_sum(msg, dst, num_segments=N)
            return out.reshape(-1, H * C) + b
        loop = jnp.arange(N, dtype=edge_index.dtype)
        src = jnp.concatenate([edge_index[0], loop])
        dst = jnp.concatenate([edge_index[1], loop])
        h = gat_layer(x, src, dst, W1, a_src1, a_dst1, b1)
        h = jax.nn.relu(h)
        out = gat_layer(h, src, dst, W2, a_src2, a_dst2, b2)
        return out

    def _L0_ffn_ref(x, W1, b1, W2, b2, s_gelu, s_out):
        import jax, jax.numpy as jnp
        import numpy as np

        def _fq(x, scale, qmin, qmax):
            q = jnp.clip(jnp.round(x / scale), qmin, qmax) * scale
            return x + jax.lax.stop_gradient(q - x)

        def _quant_weight(W):
            scale = jnp.max(jnp.abs(W)) / 127.0
            return _fq(W, scale, -127.0, 127.0)
        h = jnp.einsum('bsd,hd->bsh', x, _quant_weight(W1)) + b1
        h = jax.nn.gelu(h, approximate=False)
        h = _fq(h, s_gelu, -128.0, 127.0)
        y = jnp.einsum('bsh,dh->bsd', h, _quant_weight(W2)) + b2
        y = _fq(y, s_out, -128.0, 127.0)
        return y

    def _L1_gnn_ref(x, edge_index, W1, att_src1, att_dst1, b1, W2, att_src2, att_dst2, b2):
        import jax, jax.numpy as jnp
        import numpy as np
        N_NODES = 10000
        N_EDGES = 3125
        DIM = 768
        NEG_SLOPE = 0.2

        def gat_conv(x, src, dst, W, att_src, att_dst, bias, num_nodes):
            h = x @ W
            a_s = h @ att_src
            a_d = h @ att_dst
            e = jax.nn.leaky_relu(a_s[src] + a_d[dst], NEG_SLOPE)
            m = jax.ops.segment_max(e, dst, num_segments=num_nodes)
            e = jnp.exp(e - m[dst])
            denom = jax.ops.segment_sum(e, dst, num_segments=num_nodes)
            alpha = e / denom[dst]
            msg = alpha[:, None] * h[src]
            out = jax.ops.segment_sum(msg, dst, num_segments=num_nodes)
            return out + bias
        n = x.shape[0]
        loops = jnp.arange(n, dtype=edge_index.dtype)
        src = jnp.concatenate([edge_index[0], loops])
        dst = jnp.concatenate([edge_index[1], loops])
        h = gat_conv(x, src, dst, W1, att_src1, att_dst1, b1, n)
        h = jax.nn.relu(h)
        out = gat_conv(h, src, dst, W2, att_src2, att_dst2, b2, n)
        return out

    def _L1_ffn_ref(x, w1, b1, w2, b2, down_w, down_b, up_w, gamma, beta):
        import jax, jax.numpy as jnp
        import numpy as np
        B, S, H, D, E = (4, 64, 768, 1024, 8)
        TOP_K = 2
        EPS = 1e-08
        LN_EPS = 1e-05

        def _gelu(t):
            return jax.nn.gelu(t, approximate=False)

        def _layer_norm(t, gamma, beta):
            mu = jnp.mean(t, axis=-1, keepdims=True)
            var = jnp.mean(jnp.square(t - mu), axis=-1, keepdims=True)
            return (t - mu) * jax.lax.rsqrt(var + LN_EPS) * gamma + beta
        logits = _gelu(x @ w1 + b1) @ w2 + b2
        routing = jax.nn.softmax(logits, axis=-1)
        topv, topi = jax.lax.top_k(routing, TOP_K)
        sparse = jnp.sum(jax.nn.one_hot(topi, E, dtype=routing.dtype) * topv[..., None], axis=-2)
        sparse = sparse / (jnp.sum(sparse, axis=-1, keepdims=True) + EPS)
        z = _gelu(jnp.einsum('bsh,ehd->bsed', x, down_w) + down_b)
        expert_out = jnp.einsum('bsed,edh->bseh', z, up_w)
        moe_out = jnp.einsum('bseh,bse->bsh', expert_out, sparse)
        return _layer_norm(x + moe_out, gamma, beta)

    def _L2_gnn_ref(x, edge_index, W, b):
        import jax, jax.numpy as jnp
        import numpy as np
        N_NODES = 10000
        N_EDGES = 3125
        DIM = 768
        n = x.shape[0]
        loop = jnp.arange(n, dtype=edge_index.dtype)
        src = jnp.concatenate([edge_index[0], loop])
        dst = jnp.concatenate([edge_index[1], loop])
        deg = jax.ops.segment_sum(jnp.ones_like(dst, dtype=x.dtype), dst, num_segments=n)
        deg_inv_sqrt = jnp.where(deg > 0, jax.lax.rsqrt(deg), 0.0)
        norm = deg_inv_sqrt[src] * deg_inv_sqrt[dst]
        h = x @ W
        msg = h[src] * norm[:, None]
        out = jax.ops.segment_sum(msg, dst, num_segments=n)
        return out + b

    def _L2_ffn_ref(x, router_w, w1, b1, w2, b2):
        import jax, jax.numpy as jnp
        import numpy as np
        E, C, F, K = (8, 768, 96, 2)
        B, T, Cc = x.shape
        flat = x.reshape(-1, Cc)
        logits = flat @ router_w.T
        probs = jax.nn.softmax(logits.astype(jnp.float32), axis=-1)
        top_w, top_i = jax.lax.top_k(probs, K)
        top_w = (top_w / top_w.sum(-1, keepdims=True)).astype(x.dtype)
        out = jnp.zeros_like(flat)
        for e in range(E):
            w_e = jnp.sum(top_w * (top_i == e), axis=-1)[:, None]
            h = jax.nn.gelu(flat @ w1[e] + b1[e], approximate=False)
            out = out + w_e * (h @ w2[e] + b2[e])
        return out.reshape(B, T, Cc)

    def _L3_gnn_ref(x, edge_index, edge_type, W1, q1, k1, b1, W2, q2, k2, b2):
        import jax, jax.numpy as jnp
        import numpy as np
        NEG_SLOPE = 0.2
        EPS = 1e-16
        N_NODES = 1024
        N_EDGES = 5000
        DIM = 768
        HEADS1 = 4
        OUT1 = DIM // HEADS1
        HEADS2 = 1
        OUT2 = DIM
        N_REL = 3

        def rgat_conv(x, W, q, k, b, src, dst, etype, heads, out_ch, n_nodes):
            xr = jnp.einsum('nd,rdf->rnf', x, W)
            oi = xr[etype, dst]
            oj = xr[etype, src]
            qi = oi @ q
            kj = oj @ k
            alpha = jax.nn.leaky_relu(qi + kj, NEG_SLOPE)
            m = jax.ops.segment_max(alpha, dst, num_segments=n_nodes)
            e = jnp.exp(alpha - m[dst])
            z = jax.ops.segment_sum(e, dst, num_segments=n_nodes)
            a = e / (z[dst] + EPS)
            msg = (a[:, :, None] * oj.reshape(-1, heads, out_ch)).reshape(-1, heads * out_ch)
            out = jax.ops.segment_sum(msg, dst, num_segments=n_nodes)
            return out + b
        src, dst = (edge_index[0], edge_index[1])
        n = x.shape[0]
        h = rgat_conv(x, W1, q1, k1, b1, src, dst, edge_type, HEADS1, OUT1, n)
        h = jax.nn.elu(h)
        out = rgat_conv(h, W2, q2, k2, b2, src, dst, edge_type, HEADS2, OUT2, n)
        return out

    def _L3_ffn_ref(x, w_in, g_in, w_out, g_out):
        import jax, jax.numpy as jnp
        import numpy as np
        EPS_NORM = 1e-06
        EPS_Q = 1e-05

        def rmsnorm(x, g):
            return x * jax.lax.rsqrt(jnp.mean(x * x, axis=-1, keepdims=True) + EPS_NORM) * g

        def activation_quant(x):
            scale = 127.0 / jnp.maximum(jnp.max(jnp.abs(x), axis=-1, keepdims=True), EPS_Q)
            return jnp.clip(jnp.round(x * scale), -128, 127) / scale

        def weight_quant(w):
            scale = 1.0 / jnp.maximum(jnp.mean(jnp.abs(w)), EPS_Q)
            return jnp.clip(jnp.round(w * scale), -1, 1) / scale

        def bitlinear(x, w, g):
            x_norm = rmsnorm(x, g)
            x_q = x_norm + jax.lax.stop_gradient(activation_quant(x_norm) - x_norm)
            w_q = w + jax.lax.stop_gradient(weight_quant(w) - w)
            return jnp.einsum('bsd,od->bso', x_q, w_q)
        h = bitlinear(x, w_in, g_in)
        up, gate = jnp.split(h, 2, axis=-1)
        y = jax.nn.silu(gate) * up
        return bitlinear(y, w_out, g_out)
    edge_index = jnp.stack([src, dst])
    x = x + _L0_gnn_ref(_layernorm(x, axis=-1), edge_index, L0_gnn_W1, L0_gnn_a_src1, L0_gnn_a_dst1, L0_gnn_b1, L0_gnn_W2, L0_gnn_a_src2, L0_gnn_a_dst2, L0_gnn_b2)
    x = x + _L0_ffn_ref(_layernorm(x, axis=-1)[None], L0_ffn_W1, L0_ffn_b1, L0_ffn_W2, L0_ffn_b2, L0_ffn_s_gelu, L0_ffn_s_out)[0]
    x = x + _L1_gnn_ref(_layernorm(x, axis=-1), edge_index, L1_gnn_W1, L1_gnn_att_src1, L1_gnn_att_dst1, L1_gnn_b1, L1_gnn_W2, L1_gnn_att_src2, L1_gnn_att_dst2, L1_gnn_b2)
    x = x + _L1_ffn_ref(_layernorm(x, axis=-1)[None], L1_ffn_w1, L1_ffn_b1, L1_ffn_w2, L1_ffn_b2, L1_ffn_down_w, L1_ffn_down_b, L1_ffn_up_w, L1_ffn_gamma, L1_ffn_beta)[0]
    x = x + _L2_gnn_ref(_layernorm(x, axis=-1), edge_index, L2_gnn_W, L2_gnn_b)
    x = x + _L2_ffn_ref(_layernorm(x, axis=-1)[None], L2_ffn_router_w, L2_ffn_w1, L2_ffn_b1, L2_ffn_w2, L2_ffn_b2)[0]
    x = x + _L3_gnn_ref(_layernorm(x, axis=-1), edge_index, edge_type_3, L3_gnn_W1, L3_gnn_q1, L3_gnn_k1, L3_gnn_b1, L3_gnn_W2, L3_gnn_q2, L3_gnn_k2, L3_gnn_b2)
    x = x + _L3_ffn_ref(_layernorm(x, axis=-1)[None], L3_ffn_w_in, L3_ffn_g_in, L3_ffn_w_out, L3_ffn_g_out)[0]
    return x

_drawn_inputs = setup_inputs


def setup_inputs(seed=0):
    import zlib

    import numpy as np

    out = dict(_drawn_inputs(seed))
    spreads = {'L0_gnn_b1': (0.0, 0.1),
     'L0_gnn_b2': (0.0, 0.1),
     'L1_gnn_b1': (0.0, 0.1),
     'L1_gnn_b2': (0.0, 0.1),
     'L1_ffn_b1': (0.0, 0.1),
     'L1_ffn_b2': (0.0, 0.1),
     'L1_ffn_down_b': (0.0, 0.369),
     'L1_ffn_gamma': (1.0, 0.2),
     'L1_ffn_beta': (0.0, 0.1),
     'L2_gnn_b': (0.0, 0.1),
     'L2_ffn_b1': (0.0, 0.8),
     'L2_ffn_b2': (0.0, 0.1),
     'L3_gnn_b1': (0.0, 0.617),
     'L3_gnn_b2': (0.0, 0.1),
     'L3_ffn_g_in': (1.0, 0.6),
     'L3_ffn_g_out': (1.0, 0.6)}
    factors = {'L0_gnn_a_dst2': 4.747,
     'L0_ffn_b1': 3.0,
     'L0_ffn_b2': 2.766,
     'L1_gnn_att_dst1': 2.949,
     'L1_gnn_att_src2': 5.85,
     'L1_gnn_att_dst2': 7.529,
     'L2_ffn_w1': 3.002,
     'L2_ffn_w2': 2.76,
     'L3_gnn_q1': 8.0,
     'L3_gnn_k1': 8.0,
     'L3_gnn_q2': 8.0,
     'L3_gnn_k2': 8.0,
     'L3_ffn_w_in': 8.0,
     'L3_ffn_w_out': 8.0}
    for name, (base, spread) in spreads.items():
        noise = np.random.default_rng([zlib.crc32(name.encode()), seed]).standard_normal(out[name].shape)
        drawn = base * np.exp(spread * noise) if base else spread * noise
        out[name] = jnp.asarray(drawn.astype(out[name].dtype))
    for name, factor in factors.items():
        out[name] = (out[name] * factor).astype(out[name].dtype)
    return out
```

```python
from contextlib import ExitStack

import numpy as np
import concourse.bass as bass
from concourse import mybir

F32 = mybir.dt.float32
F32R = mybir.dt.float32r
BF16 = mybir.dt.bfloat16
F16 = mybir.dt.float16
I32 = mybir.dt.int32
U16 = mybir.dt.uint16
U32 = mybir.dt.uint32
ALU = mybir.AluOpType
ACT = mybir.ActivationFunctionType
AX = mybir.AxisListType

N = 625
Q = 125
T = N // Q
NP = N + 1
D = 768
K = D // 128
HD = D // 2
E = 10000
EC = E // Q
HALF = [(0, 314), (314, 312)]
SRC_HALF = [(0, 313), (313, 312)]
REL = 3
BANKS = 8
NEG = -1e30
SLOPE = 0.2
STAGE = 8
RMAX = bass.bass_isa.ReduceOp.max
RADD = bass.bass_isa.ReduceOp.add
MAGIC = 12582912.0
NE = 8
FF = 1024
CW = 256
NCH = FF // CW
RW = 384
F0 = 96
F3 = 64


class Signal:

    def __init__(self, name, sem, book):
        self.name, self.sem, self.book, self.n = name, sem, book, 0

    def at(self, key, by=1):
        self.n += by
        self.book[self.name, key] = self.n
        return self.sem, by

    def after(self, key):
        if "final" in self.book and (self.name, key) not in self.book:
            raise KeyError((self.name, key))
        return self.sem, self.book.get((self.name, key), 1)

    def so_far(self):
        return self.sem, self.n


def build(nc, I, out, book, scratch, upto=99):
    ctx = ExitStack()
    with ctx:
        def sb(name, shape, dt):
            return ctx.enter_context(nc.sbuf_tensor(name, shape, dt))

        signals = {}

        def sig(name):
            if name not in signals:
                signals[name] = Signal(name, ctx.enter_context(nc.semaphore(name)), book)
            return signals[name]

        x = sb("x", [Q, T, D], F32)
        tok = sb("tok", [Q, T, D], F32)
        xTh = sb("xTh", [128, K, NP], F32R)
        xTl = sb("xTl", [128, K, NP], F32R)
        Wraw = sb("Wraw", [128, 4, D], F32)
        Wh = sb("Wh", [128, K * D], F32R)
        Wl = sb("Wl", [128, K * D], F32R)
        hh = sb("hh", [128, 3880], F32R)
        hl = sb("hl", [128, 3880], F32R)
        Ph = sb("Ph", [128, T * N], F32R)
        Pl = sb("Pl", [128, T * N], F32R)
        ct = sb("ct", [Q, T, N], U16)
        mask_m = sb("mask", [Q, T * N + 1], BF16)
        mask = mask_m[:, 0:T * N].rearrange("p (t n) -> p t n", n=N)
        tmp = sb("tmp", [128, 4 * N], F32)
        bc = sb("bc", [128, 4 * N], F32)
        rows = sb("rows", [128, 2 * N], F32)
        bb = sb("bb", [Q, D], F32)
        ident = sb("ident", [128, 128], F32)
        att = sb("att", [128, 6, K, 8], F32)
        Wqh = sb("Wqh", [128, REL, K, 8], F32R)
        Wql = sb("Wql", [128, REL, K, 8], F32R)
        ac = sb("ac", [Q, REL, T, 8], F32)
        na = sb("na", [Q, REL, T, 4], F32)
        Am = sb("Am", [Q, REL, T, 4], F32)
        mm = sb("mm", [Q, T, 4], F32)
        mt = sb("mt", [Q, T, 4], F32)
        Rc = sb("Rc", [Q, REL, 2, T, 4], F32)
        dn = sb("dn", [Q, T, 4], F32)
        rd = sb("rd", [Q, T, 4], F32)
        deg = sb("deg", [Q, T], F32)
        dis = sb("dis", [Q, T], F32)
        st = sb("st", [Q, T, 2, 6], F32)
        mv = sb("mv", [Q, T, 2], F32)
        sd = sb("sd", [Q, T], F32)
        rs = sb("rs", [Q, T], F32)
        dn8 = sb("iota8", [Q, 8], I32)
        sm = sb("sm", [128, 16], F32)
        gb = sb("gb", [128, 64], F32)
        b1c = sb("b1c", [128, 4], F32)
        b2c = sb("b2c", [128, NE], F32)
        rt = sb("rt", [Q, T, 24], F32)
        PS = [ctx.enter_context(nc.psum_tensor(f"bank{b}", [128, 512], F32)) for b in range(BANKS)]

        def ttile(i):
            return tmp[:, i * N:(i + 1) * N]

        done = sig("product_done")
        consts = sig("constants")
        vstep = sig("dve_step")
        astep = sig("act_step")
        gstep = sig("pool_step")
        raw_in = [sig(f"raw_loaded{i}") for i in range(4)]
        par = sig("parameters_loaded")
        bias_in = sig("bias_loaded")
        x_in = sig("x_loaded")

        njob = [0]

        def open_job(pe, key):
            n = njob[0]
            njob[0] += 1
            book["job", key] = n
            if n >= BANKS:
                name, k = book.get(("released", n - BANKS), (None, None))
                if name:
                    pe.wait_ge(*signals[name].after(k))
            return PS[n % BANKS]

        def bank(key):
            return PS[book["job", key] % BANKS]

        def frees(key, signal, event):
            book["released", book["job", key]] = (signal.name, event)
            return signal.at(event)

        nload = {"n": 0}

        def raw_slot(key):
            return book.get(("raw", key), 0)

        def load_raw(sp, key, pieces, width=1):
            n = nload["n"]
            if n == 0:
                sp.wait_ge(*hot_ready.after(2 * REL * EC - 1))
            if n % 4 + width > 4:
                n += 4 - n % 4
            nload["n"] = n + width
            book["raw", key] = n % 4
            for j in range(width):
                book["rawuse", n + j] = key
                p = n + j - 4
                while p >= 0 and ("rawuse", p) not in book:
                    p -= 4
                for name, ev in book.get(("rawreaders", book.get(("rawuse", p))), []):
                    sp.wait_ge(*signals[name].after(ev))
            s = raw_in[n % 4]
            for i, (view, src) in enumerate(pieces):
                sp.dma_start(view(Wraw[:, n % 4:n % 4 + width, :]), src,
                             allow_slow_non_contiguous=True).then_inc(*s.at(key, 16))
            book["rawsig", key] = s.name

        def raw_reader(key, signal, event):
            l = book.setdefault(("rawreaders", key), [])
            if (signal.name, event) not in l:
                l.append((signal.name, event))
            return signal.at(event)

        def wait_raw(eng, key):
            name = book.get(("rawsig", key))
            if name:
                eng.wait_ge(*signals[name].after(key))

        def raw(key, width=1):
            s = raw_slot(key)
            return Wraw[:, s:s + width, :]

        src_d, dst_d, typ_d = I["src"], I["dst"], I["edge_type_3"]
        def edge_view(j):
            return Wraw[0:Q, j, 0:3 * EC]
        ei = edge_view(0).bitcast(I32).rearrange("p (a c) -> p a c", a=3)
        ef = edge_view(1).rearrange("p (a c) -> p a c", a=3)
        dk = edge_view(2).rearrange("p (a c) -> p a c", a=3)
        iot = tmp[0:Q, 0:N]
        iot_i = tmp[0:Q, N:2 * N].bitcast(I32)
        hotd = bc[0:Q, :].bitcast(BF16)
        hots = bc[0:Q, 2 * N:4 * N].bitcast(BF16)
        iot16 = tmp[0:Q, 2 * N:3 * N].bitcast(F16)[:, 0:N]
        hot_d = hotd[:, 0:2 * NP].rearrange("p (a b) -> p a b", a=2)
        hot_s = hots[:, 0:2 * NP].rearrange("p (a b) -> p a b", a=2)
        crel = tok[:, :, 0:N]
        ctot = x[:, :, 0:N]
        hot_ready = sig("onehot_ready")
        hot_used = sig("onehot_used")
        cnt = sig("counts")
        cnt_st = sig("counts_stored")
        cnt_ld = sig("counts_loaded")
        mask_ld = sig("mask_loaded")

        def counts_pe(pe):
            for r in range(REL):
                for hf in range(2):
                    c0, w = SRC_HALF[hf]
                    jobs = [open_job(pe, ("count", r, hf, t)) for t in range(T)]
                    for c in range(EC):
                        g = (r * 2 + hf) * EC + c
                        pe.wait_ge(*hot_ready.after(g))
                        for t in range(T):
                            m = pe.matmul(jobs[t][0:Q, 0:w], hot_d[:, g % 2, t * Q:(t + 1) * Q],
                                          hot_s[:, g % 2, 0:w], start=c == 0, stop=c == EC - 1)
                            if c == EC - 1:
                                m.then_inc(*done.at(("count", r, hf, t)))
                            elif t == T - 1:
                                m.then_inc(*hot_used.at(g))
                pe.wait_ge(*consts.after("ident"))
                for s in range(T):
                    for b, ds in enumerate(([0, 1, 2], [3, 4])):
                        ps = open_job(pe, ("ctT", r, s, b))
                        pe.wait_ge(*cnt.after(("rel", r, T - 1, 1)))
                        for i, d in enumerate(ds):
                            m = pe.transpose(ps[0:Q, i * Q:(i + 1) * Q], crel[:, d, s * Q:(s + 1) * Q], ident[0:Q, 0:Q])
                        m.then_inc(*done.at(("ctT", r, s, b)))
            for s in range(T):
                for b, ds in enumerate(([0, 1, 2], [3, 4])):
                    ps = open_job(pe, ("ctT", 3, s, b))
                    pe.wait_ge(*cnt.after("total"))
                    for i, d in enumerate(ds):
                        m = pe.transpose(ps[0:Q, i * Q:(i + 1) * Q], ctot[:, d, s * Q:(s + 1) * Q], ident[0:Q, 0:Q])
                    m.then_inc(*done.at(("ctT", 3, s, b)))

        def counts_dve(v):
            v.wait_ge(*x_in.after("edges"))
            v.tensor_copy(ef, ei).then_inc(*vstep.at("ef"))
            v.wait_ge(*vstep.after("ef"))
            for r in range(REL):
                v.tensor_scalar(dk[:, r, :], ef[:, 2, :], float(r), 1000.0, ALU.not_equal, ALU.mult).then_inc(*vstep.at(("dk0", r)))
            v.wait_ge(*vstep.after(("dk0", REL - 1)))
            for r in range(REL):
                v.tensor_tensor(dk[:, r, :], dk[:, r, :], ef[:, 1, :], ALU.add).then_inc(*vstep.at(("dk", r)))
            v.wait_ge(*consts.after("iota"))
            v.tensor_copy(iot16, iot_i).then_inc(*vstep.at("iota16"))
            v.wait_ge(*vstep.after("iota16"))
            for r in range(REL):
                for hf in range(2):
                    c0, w = SRC_HALF[hf]
                    for c in range(EC):
                        g = (r * 2 + hf) * EC + c
                        if g >= 2:
                            if (g - 2) % EC == EC - 1:
                                gg = (g - 2) // EC
                                v.wait_ge(*done.after(("count", gg // 2, gg % 2, T - 1)))
                            else:
                                v.wait_ge(*hot_used.after(g - 2))
                        v.tensor_scalar(hot_d[:, g % 2, 0:N], iot16, dk[:, r, c:c + 1], None, ALU.is_equal)
                        v.tensor_scalar(hot_s[:, g % 2, 0:w], iot16[:, c0:c0 + w], ef[:, 0, c:c + 1], None,
                                        ALU.is_equal).then_inc(*hot_ready.at(g))
                    for t in range(T):
                        v.wait_ge(*done.after(("count", r, hf, t)))
                        if t == 0 and hf == 0 and r > 0:
                            v.wait_ge(*done.after(("ctT", r - 1, T - 1, 1)))
                        v.tensor_copy(crel[:, t, c0:c0 + w], bank(("count", r, hf, t))[0:Q, 0:w]).then_inc(
                            *frees(("count", r, hf, t), cnt, ("rel", r, t, hf)))
                v.wait_ge(*cnt.after(("rel", r, T - 1, 1)))
                if r > 0:
                    v.wait_ge(*cnt_st.after(("mask", r - 1)))
                v.tensor_scalar(mask[:], crel, 0.0, NEG, ALU.is_equal, ALU.mult).then_inc(*cnt.at(("mask", r)))
                if r == 0:
                    v.tensor_copy(ctot, crel).then_inc(*vstep.at(("tot", r)))
                else:
                    v.wait_ge(*vstep.after(("tot", r - 1)))
                    v.tensor_tensor(ctot, ctot, crel, ALU.add).then_inc(*vstep.at(("tot", r)))
                for s in range(T):
                    for b, (d0, dw) in enumerate(((0, 3), (3, 2))):
                        v.wait_ge(*done.after(("ctT", r, s, b)))
                        if r > 0 and s == 0 and b == 0:
                            v.wait_ge(*cnt_st.after(("ct", r - 1)))
                        v.tensor_copy(ct[:, s, d0 * Q:(d0 + dw) * Q], bank(("ctT", r, s, b))[0:Q, 0:dw * Q]).then_inc(
                            *frees(("ctT", r, s, b), cnt, ("ct", r, s, b)))
            v.wait_ge(*vstep.after(("tot", REL - 1)))
            v.wait_ge(*consts.after("ident"))
            for t in range(T):
                m = v.tensor_tensor(ctot[:, t, t * Q:(t + 1) * Q], ctot[:, t, t * Q:(t + 1) * Q], ident[0:Q, 0:Q], ALU.add)
            m.then_inc(*cnt.at("total"))
            v.wait_ge(*cnt.after("total"))
            v.wait_ge(*cnt_st.after(("mask", REL - 1)))
            v.tensor_scalar(mask[:], ctot, 0.0, NEG, ALU.is_equal, ALU.mult).then_inc(*cnt.at(("mask", 3)))
            v.tensor_reduce(deg[:], ctot, AX.X, ALU.add).then_inc(*cnt.at("deg"))
            for s in range(T):
                for b, (d0, dw) in enumerate(((0, 3), (3, 2))):
                    v.wait_ge(*done.after(("ctT", 3, s, b)))
                    if s == 0 and b == 0:
                        v.wait_ge(*cnt_st.after(("ct", REL - 1)))
                    v.tensor_copy(ct[:, s, d0 * Q:(d0 + dw) * Q], bank(("ctT", 3, s, b))[0:Q, 0:dw * Q]).then_inc(
                        *frees(("ctT", 3, s, b), cnt, ("ct", 3, s, b)))

        def counts_sp(sp):
            for i, a in enumerate((src_d, dst_d, typ_d)):
                sp.dma_start(ei[:, i, :], a.rearrange("(p c) -> p c", c=EC)).then_inc(*x_in.at("edges", 16))

        def counts_store(sp):
            for r in range(REL):
                sp.wait_ge(*cnt.after(("mask", r)))
                sp.dma_start(scratch["mask"][r].rearrange("(t p) n -> p t n", p=Q), mask[:]).then_inc(*cnt_st.at(("mask", r), 16))
                sp.wait_ge(*cnt.after(("ct", r, T - 1, 1)))
                sp.wait_ge(*cnt_st.after(("mask", r)))
                sp.dma_start(scratch["ct"][r].rearrange("(t p) n -> p t n", p=Q), ct[:]).then_inc(*cnt_st.at(("ct", r), 16))
                sp.wait_ge(*cnt_st.after(("ct", r)))
            sp.wait_ge(*cnt.after("deg"))
            sp.wait_ge(*cnt.after(("mask", 3)))
            sp.dma_start(scratch["mask"][REL].rearrange("(t p) n -> p t n", p=Q), mask[:]).then_inc(*cnt_st.at(("mask", REL), 16))
            sp.wait_ge(*done.after(("ctT", 3, T - 1, 1)))
            sp.dma_start(x[:], I["x"].rearrange("(t p) d -> p t d", p=Q)).then_inc(*x_in.at("x", 16))

        def consts_pool(g):
            g.iota(iot_i, pattern=[[1, N]], base=0, channel_multiplier=0).then_inc(*consts.at("iota"))
            g.iota(dn8[:], pattern=[[1, 8]], base=0, channel_multiplier=0).then_inc(*consts.at("iota8"))
            g.memset(ident[:], 0.0).then_inc(*gstep.at("id0"))
            g.memset(att[:], 0.0).then_inc(*consts.at("att0"))
            g.wait_ge(*gstep.after("id0"))
            g.affine_select(out=ident[:], in_=ident[:], compare_op=ALU.not_equal, fill=1.0, base=0,
                            pattern=[[-1, 128]], channel_multiplier=1).then_inc(*consts.at("ident"))
            g.memset(xTh[:, :, N:NP].bitcast(F32), 0.0).then_inc(*consts.at("pad"))
            g.memset(xTl[:, :, N:NP].bitcast(F32), 0.0).then_inc(*consts.at("pad"))

        def params_sp(sp):
            sp.wait_ge(*consts.after("att0"))

            def p(dst, src):
                sp.dma_start(dst, src, allow_slow_non_contiguous=True).then_inc(*par.at("all", 16))
            C = D // 4
            for i, (a, b) in enumerate((("L0_gnn_a_src1", "L0_gnn_a_dst1"), ("L0_gnn_a_src2", "L0_gnn_a_dst2"))):
                for which, name in enumerate((a, b)):
                    for h in range(4):
                        f = h * C
                        while f < (h + 1) * C:
                            e = min((f // 128 + 1) * 128, (h + 1) * C)
                            p(att[f % 128:f % 128 + e - f, i, f // 128, which * 4 + h:which * 4 + h + 1],
                              I[name][h, f - h * C:e - h * C].rearrange("(p a) -> p a", a=1))
                            f = e
            for i, (a, b) in ((2, ("L1_gnn_att_src1", "L1_gnn_att_dst1")), (3, ("L1_gnn_att_src2", "L1_gnn_att_dst2"))):
                for which, name in enumerate((a, b)):
                    p(att[:, i, :, which:which + 1], I[name].rearrange("(j p a) -> p j a", p=128, a=1))
            for which, name in enumerate(("L3_gnn_k1", "L3_gnn_q1")):
                p(att[:, 4, :, which * 4:which * 4 + 4], I[name].rearrange("(j p) a -> p j a", p=128))
            for which, name in enumerate(("L3_gnn_k2", "L3_gnn_q2")):
                p(att[:, 5, :, which:which + 1], I[name].rearrange("(j p) a -> p j a", p=128))
            p(b1c[:, 0:3], I["L1_ffn_b1"].rearrange("(j p) -> p j", p=128))
            p(b1c[0:F0, 3:4], I["L0_ffn_b1"].rearrange("(p a) -> p a", a=1))
            p(b2c[0:F0, :], I["L2_ffn_b1"].rearrange("e p -> p e"))
            p(gb[:], I["L1_ffn_down_b"].rearrange("e (j p) -> p (e j)", p=128))
            p(sm[:, 0:1], I["L0_ffn_s_gelu"].partition_broadcast(128))
            p(sm[:, 1:2], I["L0_ffn_s_out"].partition_broadcast(128))

        xr = sig("x_ready")
        lnv = sig("norm_step")
        lna = sig("norm_root")
        tokr = sig("tok_ready")
        xTa = sig("xT_high")
        xTv = sig("xT_low")
        tok_last = {}

        def norm_dve(v, i, x_event, tok_free, src=None, dst=None, eps=1e-5, gamma=False):
            src = x if src is None else src
            dst = tok if dst is None else dst
            for t in range(T):
                for e in x_event(t):
                    v.wait_ge(*e)
                for hf in range(2):
                    m = v.bn_stats(st[:, t, hf, :], src[:, t, hf * HD:(hf + 1) * HD])
                m.then_inc(*lnv.at((i, "st", t)))
            for t in range(T):
                v.wait_ge(*lnv.after((i, "st", t)))
                m = v.bn_aggr(mv[:, t, :], st[:, t, :, :])
            m.then_inc(*lnv.at((i, "mv")))
            v.wait_ge(*lnv.after((i, "mv")))
            v.tensor_scalar(sd[:], mv[:, :, 1], eps, None, ALU.add).then_inc(*lnv.at((i, "sd")))
            v.wait_ge(*lna.after(i))
            v.reciprocal(rs[:], sd[:]).then_inc(*lnv.at((i, "rs")))
            v.wait_ge(*lnv.after((i, "rs")))
            for e in tok_free():
                v.wait_ge(*e)
            for t in range(T):
                v.tensor_scalar(dst[:, t, :], src[:, t, :], mv[:, t, 0:1], rs[:, t:t + 1], ALU.subtract,
                                ALU.mult).then_inc(*tokr.at((i, t)))

        def norm_act(a, i):
            a.wait_ge(*lnv.after((i, "sd")))
            a.activation(sd[:], sd[:], ACT.Sqrt).then_inc(*lna.at(i))

        def turn_pe(pe, i, ready):
            pe.wait_ge(*consts.after("ident"))
            for t in range(T):
                pe.wait_ge(*ready(t))
                for b in range(2):
                    ps = open_job(pe, ("turn", i, t, b))
                    for j in range(3):
                        k = 3 * b + j
                        m = pe.transpose(ps[:, j * Q:(j + 1) * Q], tok[:, t, k * 128:(k + 1) * 128], ident[0:Q, 0:Q])
                    m.then_inc(*done.at(("turn", i, t, b)))

        def turn_act(a, i, xT_free):
            for e in xT_free():
                a.wait_ge(*e)
            for t in range(T):
                for b in range(2):
                    a.wait_ge(*done.after(("turn", i, t, b)))
                    a.activation(xTh[:, 3 * b:3 * b + 3, t * Q:(t + 1) * Q],
                                 bank(("turn", i, t, b))[:, 0:3 * Q].rearrange("p (j q) -> p j q", q=Q),
                                 ACT.Copy).then_inc(*xTa.at((i, t, b)))

        def turn_dve(v, i, xT_free):
            for e in xT_free():
                v.wait_ge(*e)
            for t in range(T):
                for b in range(2):
                    v.wait_ge(*xTa.after((i, t, b)))
                    v.tensor_tensor(xTl[:, 3 * b:3 * b + 3, t * Q:(t + 1) * Q],
                                    bank(("turn", i, t, b))[:, 0:3 * Q].rearrange("p (j q) -> p j q", q=Q),
                                    xTh[:, 3 * b:3 * b + 3, t * Q:(t + 1) * Q].bitcast(F32),
                                    ALU.subtract).then_inc(*frees(("turn", i, t, b), xTv, (i, t, b)))

        def xT_whole(i):
            return xTv.after((i, T - 1, 1))

        def pairs(high, low):
            return [(high[0], high[1]), (high[0], low[1]), (low[0], high[1])]

        wqa = sig("WT_ready")
        wqr = sig("Wq_ready")
        whi = sig("W_high")
        wlo = sig("W_low")
        aca = sig("att_terms")
        rowa = sig("rows_ready")
        bcg = sig("broadcast_done")
        asu = sig("row_used_dve")
        r2u = sig("row_used_act")
        agv = sig("att_step")
        pn2 = sig("P_n2")
        pd = sig("P_diff")
        pe_ = sig("P_exp")
        pv = sig("P_value")
        ph = sig("P_high")
        pl = sig("P_low")
        plc = sig("counts_low")

        def pl_after(key):
            return (plc if L[key[0]].att is None else pl).after(key)

        pu = sig("P_used")
        hia = sig("h_high")
        hiv = sig("h_low")
        onesg = sig("h_ones")
        agr = sig("agg_read")
        bx = sig("x_with_bias")
        elu = sig("elu")

        class Layer:
            def __init__(s, i, turn, heads, rels, W, attn, bias, last, act):
                s.i, s.turn, s.H, s.R, s.W, s.att, s.bias, s.last, s.act = i, turn, heads, rels, W, attn, bias, last, act
                s.C = D // heads
                s.step = s.C + 2 if heads > 1 else HD + 4
                s.parts = heads if heads > 1 else 2

        L = [
            Layer(0, 0, 4, 1, "L0_gnn_W1", 0, "L0_gnn_b1", False, "relu"),
            Layer(1, 1, 4, 1, "L0_gnn_W2", 1, "L0_gnn_b2", True, None),
            Layer(2, 3, 1, 1, "L1_gnn_W1", 2, "L1_gnn_b1", False, "relu"),
            Layer(3, 4, 1, 1, "L1_gnn_W2", 3, "L1_gnn_b2", True, None),
            Layer(4, 6, 1, 1, "L2_gnn_W", None, "L2_gnn_b", True, None),
            Layer(5, 8, 4, REL, "L3_gnn_W1", 4, "L3_gnn_b1", False, "elu"),
            Layer(6, 9, 1, REL, "L3_gnn_W2", 5, "L3_gnn_b2", True, None),
        ]

        def w_src(l, r, k):
            w = I[l.W] if l.R == 1 else I[l.W][r]
            return w[k * 128:(k + 1) * 128, :]

        def gnn_sp(sp, l):
            if l.R > 1:
                for r in range(l.R):
                    for k in range(K):
                        load_raw(sp, ("q", l.i, r, k), [(lambda v: v[:, 0, :], w_src(l, r, k))])
            def load_mask(r):
                sp.wait_ge(*mask_free(l, r))
                sp.dma_start(mask[:], scratch["mask"][r if l.R > 1 else REL].rearrange("(t p) n -> p t n", p=Q)).then_inc(
                    *mask_ld.at(("mask", l.i, r), 16))
            if l.R > 1:
                load_mask(0)
            def load_counts(r):
                for e in ct_free(l, r):
                    sp.wait_ge(*e)
                sp.dma_start(ct[:], scratch["ct"][r].rearrange("(t p) n -> p t n", p=Q)).then_inc(
                    *cnt_ld.at(("ct", l.i, r), 16))
            if l.R > 1:
                load_counts(0)
            for r in range(l.R):
                for k in range(K):
                    load_raw(sp, ("w", l.i, r, k), [(lambda v: v[:, 0, :], w_src(l, r, k))])
                if r == 0:
                    load_bias(sp, ("b", l.i), l.bias)
                    if l.R > 1:
                        load_mask(1)
                        load_mask(2)
                    elif l.i > 0 and l.att is not None:
                        load_mask(0)
                else:
                    load_counts(r)

        def load_bias(sp, key, name):
            n = BIASES.index(key)
            if n > 0:
                prev = BIASES[n - 1]
                if prev[0] == "b":
                    p = L[prev[1]]
                    sp.wait_ge(*(bx.after((p.i, T - 1)) if p.last else agr.after(last_agg(p))))
                else:
                    sp.wait_ge(*fv.after(prev))
            sp.dma_start(bb[:], I[name].partition_broadcast(Q)).then_inc(*bias_in.at(key, 16))

        BIASES = [("b", 0), ("b", 1), ("f0", "bias"), ("b", 2), ("b", 3), ("f1", "gamma"), ("b", 4), ("b", 5),
                  ("b", 6), ("f3", "g")]
        fv = sig("ffn_dve")
        fa = sig("ffn_act")
        fg = sig("ffn_pool")
        fd = sig("ffn_loaded")

        def last_agg(p):
            return (p.i, "fin", T - 1, p.parts - 1)

        def mask_free(l, r):
            if r > 0:
                return agv.after((l.i, "A", r - 1, l.H - 1, T - 1))
            p = [z for z in L[:l.i] if z.att is not None][-1]
            return pl_after((p.i, p.R - 1, p.H - 1, T - 1))

        def ct_free(l, r):
            if r > 0:
                return [pv.after((l.i, r - 1, l.H - 1, T - 1))]
            if l.i == 5:
                return [pl_after((4, 0, 0, T - 1))]
            return [pv.after((l.i - 1, REL - 1, L[l.i - 1].H - 1, T - 1))]

        def wq_pe(pe, l, r):
            src = "q" if l.R > 1 else "w"
            n2 = 2 * l.H
            pe.wait_ge(*consts.after("ident"))
            pe.wait_ge(*par.after("all"))

            def turn(k):
                wait_raw(pe, (src, l.i, r, k))
                for b in range(2):
                    ps = open_job(pe, ("wT", l.i, r, k, b))
                    for j in range(3):
                        f = 3 * b + j
                        m = pe.transpose(ps[:, j * 128:(j + 1) * 128], raw((src, l.i, r, k))[:, 0, f * 128:(f + 1) * 128], ident[:, :])
                    m.then_inc(*(raw_reader((src, l.i, r, k), done, ("wT", l.i, r, k, b)) if b == 1
                                 else done.at(("wT", l.i, r, k, b))))

            def product(k):
                for b in range(2):
                    pe.wait_ge(*wqa.after((l.i, r, k, b)))
                ps = bank(("wT", l.i, r, k, 1))
                for b in range(2):
                    for j in range(3):
                        f = 3 * b + j
                        m = pe.matmul(ps[:, 400:400 + n2], wt_buf(r, k, b)[:, j * 128:(j + 1) * 128],
                                      att[:, l.att, f, 0:n2], start=f == 0, stop=f == K - 1)
                m.then_inc(*done.at(("wqp", l.i, r, k)))
            for k in range(K + 2):
                if k < K:
                    turn(k)
                if k > 1:
                    product(k - 2)

        def wt_buf(r, k, b):
            i = (r * K + k) % 3 * 2 + b
            return tmp[:, i * HD:(i + 1) * HD]

        def wq_act(a, l, r, tmp_free):
            for e in tmp_free():
                a.wait_ge(*e)
            n2 = 2 * l.H

            def high(k):
                a.wait_ge(*done.after(("wqp", l.i, r, k)))
                if l.i > 0 and r == 0 and k == 0:
                    p = [z for z in L[:l.i] if z.att is not None][-1]
                    a.wait_ge(*done.after(("col", p.i, p.R - 1)))
                a.activation(Wqh[:, r, k, 0:n2], bank(("wT", l.i, r, k, 1))[:, 400:400 + n2], ACT.Copy).then_inc(
                    *wqr.at(("h", l.i, r, k)))
            for k in range(K + 2):
                if k < K:
                    for b in range(2):
                        a.wait_ge(*done.after(("wT", l.i, r, k, b)))
                        if r * K + k > 2:
                            a.wait_ge(*done.after(("wqp", l.i) + divmod(r * K + k - 3, K)))
                        m = a.activation(wt_buf(r, k, b), bank(("wT", l.i, r, k, b))[:, 0:384], ACT.Copy)
                        m.then_inc(*(frees(("wT", l.i, r, k, b), wqa, (l.i, r, k, b)) if b == 0 else wqa.at((l.i, r, k, b))))
                if k > 1:
                    high(k - 2)
                if l.R == 1 and k < K:
                    split_act(a, l, 0, [k])

        def wq_dve(v, l, r):
            n2 = 2 * l.H
            for k in range(K):
                v.wait_ge(*wqr.after(("h", l.i, r, k)))
                v.tensor_tensor(Wql[:, r, k, 0:n2], bank(("wT", l.i, r, k, 1))[:, 400:400 + n2],
                                Wqh[:, r, k, 0:n2].bitcast(F32), ALU.subtract).then_inc(
                    *frees(("wT", l.i, r, k, 1), wlq, ("l", l.i, r) if k == K - 1 else ("l", l.i, r, k)))

        wlq = sig("Wq_low")

        def split_act(a, l, r, ks=range(K)):
            for k in ks:
                wait_raw(a, ("w", l.i, r, k))
                if k == 0:
                    for e in w_free(l, r):
                        a.wait_ge(*e)
                a.activation(Wh[:, k * D:(k + 1) * D], raw(("w", l.i, r, k))[:, 0, :], ACT.Copy).then_inc(
                    *raw_reader(("w", l.i, r, k), whi, (l.i, r, k)))

        def next_weights(l, r, n):
            every, first = (3, 2) if l.H > 1 else (1, 0)
            return [n // every] if r + 1 < l.R and n % every == first and n // every < K else []

        def split_pool(g, l, r, ks=range(K)):
            if len(ks) > 0:
                pool_wait(g)
            for k in ks:
                g.wait_ge(*whi.after((l.i, r, k)))
                g.tensor_tensor(Wl[:, k * D:(k + 1) * D], raw(("w", l.i, r, k))[:, 0, :],
                                Wh[:, k * D:(k + 1) * D].bitcast(F32), ALU.subtract).then_inc(
                    *pool_event(wlo, (l.i, r, k), raw_reader(("w", l.i, r, k), wlo, (l.i, r, k))))

        w_last = {}

        def w_free(l, r):
            if r > 0:
                return [done.after(("lin", l.i, r - 1, T - 1, 1))]
            if l.i == 0:
                return []
            p = L[l.i - 1]
            return [done.after(("lin", p.i, p.R - 1, T - 1, 1))] + [e() for e in w_last.get(l.i, [])]

        def col_pe(pe, l, r):
            n2 = 2 * l.H
            pe.wait_ge(*xT_whole(l.turn))
            pe.wait_ge(*wlq.after(("l", l.i, r)))
            ps = open_job(pe, ("col", l.i, r))
            for t in range(T):
                for k in range(K):
                    for n, (s_, m_) in enumerate(pairs((xTh, Wqh), (xTl, Wql))):
                        m = pe.matmul(ps[0:Q, t * 8:t * 8 + n2], s_[:, k, t * Q:(t + 1) * Q], m_[:, r, k, 0:n2],
                                      start=k == 0 and n == 0, stop=k == K - 1 and n == 2)
            m.then_inc(*done.at(("col", l.i, r)))

        def col_act(a, l, r):
            a.wait_ge(*done.after(("col", l.i, r)))
            n2 = 2 * l.H
            for e in att_free(l, r):
                a.wait_ge(*e)
            a.activation(ac[:, r, :, 0:n2], bank(("col", l.i, r))[0:Q, 0:T * 8].rearrange("p (t c) -> p t c", c=8)[:, :, 0:n2],
                         ACT.Copy).then_inc(*frees(("col", l.i, r), aca, (l.i, r)))

        def att_free(l, r):
            if l.i == 0 or r > 0:
                return []
            p = [z for z in L[:l.i] if z.att is not None][-1]
            return [pd.after((p.i, p.R - 1, p.H - 1, T - 1)), pn2.after((p.i, p.R - 1, p.H - 1, T - 1))]

        def na_dve(v, l, r):
            v.wait_ge(*aca.after((l.i, r)))
            if r == 0 and l.i > 0:
                p = [z for z in L[:l.i] if z.att is not None][-1]
                v.wait_ge(*pn2.after((p.i, p.R - 1, p.H - 1, T - 1)))
            v.tensor_scalar(na[:, r, :, 0:l.H], ac[:, r, :, 0:l.H], -SLOPE, None, ALU.mult).then_inc(*agv.at((l.i, "na", r)))

        spr = sig("columns_spread")

        def spread_dve(v, key, cols, slot, l, free):
            for e in free:
                v.wait_ge(*e)
            if l.H == 1:
                return
            dst = ttile(slot)[0:Q, :].rearrange("p (t c) -> p t c", c=Q)
            v.tensor_copy(dst[:, :, 0:96].rearrange("p t (h c) -> p t h c", c=32),
                          cols[:, :, 0:3].unsqueeze(3).to_broadcast([Q, T, 3, 32]))
            v.tensor_copy(dst[:, :, 96:97], cols[:, :, 3:4]).then_inc(*spr.at(key))

        def turnrow_pe(pe, key, cols, slot, l, ready):
            m1 = 97 if l.H > 1 else 1
            dst = ttile(slot)[0:Q, :].rearrange("p (t c) -> p t c", c=Q)
            for b, ts in enumerate(([0, 1, 2], [3, 4])):
                ps = open_job(pe, ("row", key, b))
                if b == 0:
                    pe.wait_ge(*(spr.after(key) if l.H > 1 else ready))
                for i, t in enumerate(ts):
                    src = dst[:, t, 0:97] if l.H > 1 else cols[:, t, 0:1]
                    m = pe.transpose(ps[0:m1, i * Q:(i + 1) * Q], src, ident[0:Q, 0:Q])
                m.then_inc(*done.at(("row", key, b)))

        def turnrow_act(a, key, slot, l, free):
            m1 = 97 if l.H > 1 else 1
            for e in free:
                a.wait_ge(*e)
            for b, (t0, w) in enumerate(((0, 3), (3, 2))):
                a.wait_ge(*done.after(("row", key, b)))
                a.activation(rows[0:m1, slot * N + t0 * Q:slot * N + (t0 + w) * Q], bank(("row", key, b))[0:m1, 0:w * Q],
                             ACT.Copy).then_inc(*frees(("row", key, b), rowa, (key, b)))

        nbc = [0]
        pool_last = {}

        def pool_event(signal, event, at=None):
            pool_last["e"] = (signal, event)
            return at or signal.at(event)

        def pool_wait(g):
            if "e" in pool_last:
                g.wait_ge(*pool_last["e"][0].after(pool_last["e"][1]))

        def broadcast(g, key, slot, h, H):
            n = nbc[0]
            nbc[0] += 1
            book["bc", key] = n % 4
            book["bckey", n] = key
            if n >= 4:
                rel = book.get(("bcfree", book["bckey", n - 4]))
                if rel:
                    g.wait_ge(*signals[rel[0]].after(rel[1]))
            h32 = 32 * h
            pool_wait(g)
            g.partition_broadcast(bc[:, (n % 4) * N:(n % 4 + 1) * N], rows[h32:h32 + 1, slot * N:(slot + 1) * N],
                                  128).then_inc(*pool_event(bcg, key))

        def brow(key):
            s = book.get(("bc", key), 0)
            return bc[0:Q, s * N:(s + 1) * N]

        def bc_reader(key, signal, event):
            book["bcfree", key] = (signal.name, event)
            return signal.at(event)

        def max_dve(v, l, r):
            for h in range(l.H):
                v.wait_ge(*bcg.after(("as", l.i, r, h)))
                if h == 0:
                    if l.i == 0:
                        v.wait_ge(*cnt.after(("mask", 3)))
                    else:
                        v.wait_ge(*mask_ld.after(("mask", l.i, r)))
                for t in range(T):
                    if h + t > 0:
                        v.wait_ge(*agv.after((l.i, "A", r, h if t else h - 1, t - 1 if t else T - 1)))
                    m = v.tensor_tensor_reduce(out=ttile(0)[0:Q, :], in0=mask[:, t, :], in1=brow(("as", l.i, r, h)),
                                               scale=1.0, scalar=-3e38, op0=ALU.add, op1=ALU.max,
                                               accum_out=Am[:, r, t, h:h + 1])
                    if t < T - 1:
                        m.then_inc(*agv.at((l.i, "A", r, h, t)))
                    else:
                        m.then_inc(*bc_reader(("as", l.i, r, h), agv, (l.i, "A", r, h, t)))
                    steps = l.R * l.H * T
                    for job in range(2 * T):
                        if -((job + 1) * steps // (-2 * T)) == (r * l.H + h) * T + t + 1:
                            lin_dve(v, l, 0, job // 2, job % 2)

        def tmp01_free(l):
            p = L[l.i - 1]
            return pl_after((p.i, p.R - 1, p.H - 1, T - 1))

        def m_dve(v, l):
            H = l.H
            v.wait_ge(*agv.after((l.i, "A", l.R - 1, H - 1, T - 1)))
            for r in range(l.R):
                v.tensor_tensor(mt[:, :, 0:H], Am[:, r, :, 0:H], ac[:, r, :, H:2 * H], ALU.add).then_inc(*agv.at((l.i, "q", r)))
                v.wait_ge(*agv.after((l.i, "q", r)))
                dst = mm if r == 0 else Am[:, r, :, :]
                v.scalar_tensor_tensor(dst[:, :, 0:H], mt[:, :, 0:H], SLOPE, mt[:, :, 0:H], ALU.mult, ALU.max).then_inc(
                    *agv.at((l.i, "l", r)))
                v.wait_ge(*agv.after((l.i, "l", r)))
                if r > 0:
                    v.tensor_tensor(mm[:, :, 0:H], mm[:, :, 0:H], Am[:, r, :, 0:H], ALU.max).then_inc(*agv.at((l.i, "m", r)))
                    v.wait_ge(*agv.after((l.i, "m", r)))
            for r in range(l.R):
                v.tensor_tensor(Rc[:, r, 0, :, 0:H], mm[:, :, 0:H], ac[:, r, :, H:2 * H], ALU.subtract)
                v.scalar_tensor_tensor(Rc[:, r, 1, :, 0:H], ac[:, r, :, H:2 * H], -SLOPE, mm[:, :, 0:H], ALU.mult,
                                       ALU.add).then_inc(*agv.at((l.i, "R", r)))

        def lin_pe(pe, l, r, jobs):
            pe.wait_ge(*xT_whole(l.turn))
            pe.wait_ge(*consts.after("pad"))
            for t, hf in jobs:
                ps = open_job(pe, ("lin", l.i, r, t, hf))
                for k in range(K):
                    if t == 0 and hf == 0:
                        pe.wait_ge(*wlo.after((l.i, r, k)))
                    for n, (s_, m_) in enumerate(pairs((xTh, Wh), (xTl, Wl))):
                        m = pe.matmul(ps[0:Q, 0:HD], s_[:, k, t * Q:(t + 1) * Q],
                                      m_[:, k * D + hf * HD:k * D + (hf + 1) * HD],
                                      start=k == 0 and n == 0, stop=k == K - 1 and n == 2)
                m.then_inc(*done.at(("lin", l.i, r, t, hf)))

        def hview(buf, l, t, hf):
            base = t * 776 + hf * (HD + 4)
            if l.H > 1:
                return buf[0:Q, base:base + HD + 4].rearrange("p (h c) -> p h c", h=2)[:, :, 0:l.C]
            return buf[0:Q, base:base + HD]

        def bview(ps, l):
            return ps[0:Q, 0:HD].rearrange("p (h c) -> p h c", h=2) if l.H > 1 else ps[0:Q, 0:HD]

        def h_free(l, r):
            if r > 0:
                return [agg_end(l, r - 1)]
            if l.i == 0:
                return []
            return [agg_end(L[l.i - 1], L[l.i - 1].R - 1)] + [e() for e in h_last.get(l.i, [])]

        h_last = {}

        def agg_end(l, r):
            return done.after(("agg", l.i, r, l.H - 1 if l.H > 1 else 0, T - 1, 0 if l.H > 1 else 1))

        def lin_act(a, l, r, t, hf):
            a.wait_ge(*done.after(("lin", l.i, r, t, hf)))
            if t == 0 and hf == 0:
                for e in h_free(l, r):
                    a.wait_ge(*e)
            if l.att is None:
                a.wait_ge(*agv.after("dis"))
                a.activation(hview(hh, l, t, hf), bview(bank(("lin", l.i, r, t, hf)), l), ACT.Copy,
                             scale=dis[:, t:t + 1]).then_inc(*hia.at((l.i, r, t, hf)))
            else:
                a.activation(hview(hh, l, t, hf), bview(bank(("lin", l.i, r, t, hf)), l), ACT.Copy).then_inc(
                    *hia.at((l.i, r, t, hf)))

        def lin_dve(v, l, r, t, hf):
            v.wait_ge(*hia.after((l.i, r, t, hf)))
            key = ("lin", l.i, r, t, hf)
            if l.att is None:
                v.scalar_tensor_tensor(hview(hl, l, t, hf), bview(bank(key), l), dis[:, t:t + 1],
                                       hview(hh, l, t, hf).bitcast(F32), ALU.mult, ALU.subtract).then_inc(
                    *frees(key, hiv, (l.i, r, t, hf)))
            else:
                v.tensor_tensor(hview(hl, l, t, hf), bview(bank(key), l), hview(hh, l, t, hf).bitcast(F32),
                                ALU.subtract).then_inc(*frees(key, hiv, (l.i, r, t, hf)))

        def ones_pool(g, l):
            for e in h_free(l, 0):
                g.wait_ge(*e)
            step = l.C + 2 if l.H > 1 else 776
            first = l.C if l.H > 1 else HD
            n = l.H if l.H > 1 else 1
            for t in range(T):
                for i in range(n):
                    c = t * 776 + first + i * step
                    g.memset(hh[0:Q, c:c + 1].bitcast(F32), 1.0)
                    g.memset(hh[0:Q, c + 1:c + 2].bitcast(F32), 0.0)
                    m = g.memset(hl[0:Q, c:c + 2].bitcast(F32), 0.0)
            m.then_inc(*pool_event(onesg, l.i))

        def pcount(l, r, h):
            n = 0
            for z in L:
                if z.i == l.i:
                    return n + r * z.H + h
                n += z.R * z.H

        def ptile_free(l, r, h, s):
            c = pcount(l, r, h) - 1
            if c < 0:
                return []
            for z in L:
                if c < z.R * z.H:
                    r0, h0 = divmod(c, z.H)
                    if z.i != l.i and l.i in p_last:
                        return [e() for e in p_last[l.i]]
                    if z.H > 1:
                        return [pu.after((z.i, r0, h0, s)) if s < T - 1 else done.after(("agg", z.i, r0, h0, T - 1, 0))]
                    return [done.after(("agg", z.i, r0, 0, T - 1, 1))]
                c -= z.R * z.H

        p_last = {}

        def prow(buf, s):
            return buf[0:Q, s * N:(s + 1) * N]

        def p_act_first(a, l, r, h, s):
            if l.att is None:
                a.wait_ge(*cnt.after(("ct", 3, T - 1, 1)))
                for e in ptile_free(l, r, h, s):
                    a.wait_ge(*e)
                a.activation(prow(Ph, s), ct[:, s, :], ACT.Copy).then_inc(*ph.at((l.i, r, h, s)))
                return
            if s == 0:
                a.wait_ge(*bcg.after(("R2", l.i, r, h)))
                a.wait_ge(*agv.after((l.i, "na", r)))
            for e in prev_tile(l, r, h, s, pd, back=2):
                a.wait_ge(*e)
            act_n2 = a.activation(ttile(2 + s_par(l, r, h, s))[0:Q, :], brow(("R2", l.i, r, h)), ACT.Relu,
                                  bias=na[:, r, s, h:h + 1])
            if s == T - 1:
                act_n2.then_inc(*bc_reader(("R2", l.i, r, h), pn2, (l.i, r, h, s)))
            else:
                act_n2.then_inc(*pn2.at((l.i, r, h, s)))

        spare = mask_m[:, 0:4 * N + 2].bitcast(F32)

        def n1_row(l, r, h, s):
            i = ((r * l.H + h) * T + s) % 4
            return ttile(i)[0:Q, :] if i < 2 else spare[:, (i - 2) * N:(i - 1) * N]

        def s_par(l, r, h, s):
            return (((r * l.H + h) * T + s)) % 2

        def prev_tile(l, r, h, s, signal, back):
            n = (r * l.H + h) * T + s - back
            if n < 0:
                return []
            c, s0 = divmod(n, T)
            r0, h0 = divmod(c, l.H)
            return [signal.after((l.i, r0, h0, s0))]

        def p_dve_diff(v, l, r, h, s):
            if l.att is None:
                return
            if s == 0:
                v.wait_ge(*bcg.after(("R1", l.i, r, h)))
            for e in prev_tile(l, r, h, s, pl, 4):
                v.wait_ge(*e)
            if l.i == 0 and (h, s) == (0, 0):
                v.wait_ge(*cnt_st.after(("mask", REL)))
            n1 = n1_row(l, r, h, s)
            ins = v.tensor_scalar(n1, brow(("R1", l.i, r, h)), ac[:, r, s, h:h + 1], 0.0, ALU.subtract, ALU.max)
            if s == T - 1:
                ins.then_inc(*bc_reader(("R1", l.i, r, h), agv, (l.i, "n1", r, h, s)))
            else:
                ins.then_inc(*agv.at((l.i, "n1", r, h, s)))
            v.wait_ge(*agv.after((l.i, "n1", r, h, s)))
            v.wait_ge(*pn2.after((l.i, r, h, s)))
            v.tensor_tensor(n1, n1, ttile(2 + s_par(l, r, h, s))[0:Q, :], ALU.min).then_inc(*pd.at((l.i, r, h, s)))

        def p_act_exp(a, l, r, h, s):
            if l.att is None:
                return
            a.wait_ge(*pd.after((l.i, r, h, s)))
            a.activation(n1_row(l, r, h, s), n1_row(l, r, h, s), ACT.Exp,
                         scale=-1.0).then_inc(*pe_.at((l.i, r, h, s)))

        def p_dve_value(v, l, r, h, s):
            if l.att is None:
                v.wait_ge(*ph.after((l.i, r, h, s)))
                v.tensor_tensor(prow(Pl, s), ct[:, s, :], prow(Ph, s).bitcast(F32), ALU.subtract).then_inc(*plc.at((l.i, r, h, s)))
                return
            v.wait_ge(*pe_.after((l.i, r, h, s)))
            if s == 0 and h == 0:
                v.wait_ge(*(cnt_ld.after(("ct", l.i, r)) if l.R > 1 else cnt.after(("ct", 3, T - 1, 1))))
            v.tensor_tensor(n1_row(l, r, h, s), n1_row(l, r, h, s), ct[:, s, :], ALU.mult).then_inc(*pv.at((l.i, r, h, s)))

        def p_act_high(a, l, r, h, s):
            if l.att is None:
                return
            a.wait_ge(*pv.after((l.i, r, h, s)))
            for e in ptile_free(l, r, h, s):
                a.wait_ge(*e)
            a.activation(prow(Ph, s), n1_row(l, r, h, s), ACT.Copy).then_inc(*ph.at((l.i, r, h, s)))

        def p_pool(g, l, r, h, s):
            if l.att is None:
                return
            if s == 0:
                pool_wait(g)
            g.wait_ge(*ph.after((l.i, r, h, s)))
            g.tensor_tensor(prow(Pl, s), n1_row(l, r, h, s), prow(Ph, s).bitcast(F32), ALU.subtract).then_inc(
                *pool_event(pl, (l.i, r, h, s)))

        def agg_pe(pe, l, r):
            pe.wait_ge(*hiv.after((l.i, r, T - 1, 1)))
            pe.wait_ge(*onesg.after(l.i))
            if l.H > 1:
                for h in range(l.H):
                    banks = [open_job(pe, ("agg", l.i, r, h, d, 0)) for d in range(T)]
                    for s in range(T):
                        pe.wait_ge(*pl_after((l.i, r, h, s)))
                        for d in range(T):
                            for n, (s_, m_) in enumerate(pairs((Ph, hh), (Pl, hl))):
                                c = s * 776 + h * (l.C + 2)
                                m = pe.matmul(banks[d][0:Q, 0:l.C + 2], prow(s_, s)[:, d * Q:(d + 1) * Q],
                                              m_[0:Q, c:c + l.C + 2], start=s == 0 and n == 0,
                                              stop=s == T - 1 and n == 2)
                            if s == T - 1:
                                m.then_inc(*done.at(("agg", l.i, r, h, d, 0)))
                            elif d == T - 1:
                                m.then_inc(*pu.at((l.i, r, h, s)))
            else:
                for d in range(T):
                    for hf in range(2):
                        w = HD + 2 if hf == 0 else HD
                        ps = open_job(pe, ("agg", l.i, r, 0, d, hf))
                        for s in range(T):
                            if d == 0 and hf == 0:
                                pe.wait_ge(*pl_after((l.i, r, 0, s)))
                            for n, (s_, m_) in enumerate(pairs((Ph, hh), (Pl, hl))):
                                c = s * 776 + hf * (HD + 4)
                                m = pe.matmul(ps[0:Q, 0:w], prow(s_, s)[:, d * Q:(d + 1) * Q], m_[0:Q, c:c + w],
                                              start=s == 0 and n == 0, stop=s == T - 1 and n == 2)
                        m.then_inc(*done.at(("agg", l.i, r, 0, d, hf)))

        def agg_jobs(l, h=None):
            if l.H > 1:
                return [(d, hh_, hh_ * l.C, l.C) for hh_ in (range(l.H) if h is None else [h]) for d in range(T)]
            return [(d, hf, hf * HD, HD) for d in range(T) for hf in range(2)]

        def agg_dve(v, l, r, h=None):
            for d, part, c0, w in agg_jobs(l, h):
                key = ("agg", l.i, r, part, d, 0) if l.H > 1 else ("agg", l.i, r, 0, d, part)
                v.wait_ge(*done.after(key))
                ps = bank(key)
                has_den = l.H > 1 or part == 0
                den = part if l.H > 1 else 0
                if l.R == 1:
                    scale = dis[:, d:d + 1]
                    if l.att is not None:
                        scale = rd[:, d, den:den + 1]
                        if has_den:
                            v.reciprocal(scale, ps[0:Q, w:w + 1]).then_inc(*agv.at((l.i, "rd", d, part)))
                            v.wait_ge(*agv.after((l.i, "rd", d, part)))
                    out_, add = (x, x[:, d, c0:c0 + w]) if l.last else (tok, bb[:, c0:c0 + w])
                    if l.last:
                        v.wait_ge(*bx.after((l.i, T - 1)))
                    elif d == 0 and part == 0:
                        v.wait_ge(*bias_in.after(("b", l.i)))
                        v.wait_ge(*done.after(("turn", l.turn, T - 1, 1)))
                    ev = (l.i, "fin", d, part)
                    v.scalar_tensor_tensor(out_[:, d, c0:c0 + w], ps[0:Q, 0:w], scale, add, ALU.mult,
                                           ALU.add).then_inc(*frees(key, agr, ev))
                else:
                    if r == 0:
                        if d == 0 and part == 0:
                            v.wait_ge(*done.after(("turn", l.turn, T - 1, 1)))
                        if has_den:
                            v.tensor_copy(dn[:, d, den:den + 1], ps[0:Q, w:w + 1])
                        v.tensor_copy(tok[:, d, c0:c0 + w], ps[0:Q, 0:w]).then_inc(*frees(key, agr, (l.i, r, d, part)))
                    else:
                        v.wait_ge(*agr.after((l.i, r - 1, d, part)))
                        if has_den:
                            v.tensor_tensor(dn[:, d, den:den + 1], dn[:, d, den:den + 1], ps[0:Q, w:w + 1], ALU.add)
                        v.tensor_tensor(tok[:, d, c0:c0 + w], tok[:, d, c0:c0 + w], ps[0:Q, 0:w], ALU.add).then_inc(
                            *frees(key, agr, (l.i, r, d, part)))

        def fin_dve(v, l):
            if l.R > 1:
                nd = l.H
                jobs = agg_jobs(l)
                v.wait_ge(*agr.after((l.i, l.R - 1, jobs[-1][0], jobs[-1][1])))
                v.tensor_scalar(dn[:, :, 0:nd], dn[:, :, 0:nd], 1e-16, None, ALU.add).then_inc(*agv.at((l.i, "dn")))
                v.wait_ge(*agv.after((l.i, "dn")))
                v.reciprocal(rd[:, :, 0:nd], dn[:, :, 0:nd]).then_inc(*agv.at((l.i, "rdn")))
                v.wait_ge(*agv.after((l.i, "rdn")))
                v.wait_ge(*(bx.after((l.i, T - 1)) if l.last else bias_in.after(("b", l.i))))
                for d in range(T):
                    for part in range(l.parts):
                        w = D // l.parts
                        c0 = part * w
                        den = part if l.H > 1 else 0
                        out_, add = (x, x[:, d, c0:c0 + w]) if l.last else (tok, bb[:, c0:c0 + w])
                        v.scalar_tensor_tensor(out_[:, d, c0:c0 + w], tok[:, d, c0:c0 + w], rd[:, d, den:den + 1], add,
                                               ALU.mult, ALU.add).then_inc(*agr.at((l.i, "fin", d, part)))
            if l.act == "relu":
                for d in range(T):
                    v.wait_ge(*agr.after((l.i, "fin", d, l.parts - 1)))
                    v.tensor_scalar(tok[:, d, :], tok[:, d, :], 0.0, None, ALU.max).then_inc(*tokr.at(("act", l.i, d)))
            if l.act == "elu":
                for d in range(T):
                    v.wait_ge(*agr.after((l.i, "fin", d, l.parts - 1)))
                    e = bc[0:Q, (d % 2) * D:(d % 2 + 1) * D]
                    if d == 0:
                        v.wait_ge(*pn2.after((l.i, l.R - 1, l.H - 1, T - 1)))
                    v.tensor_scalar(e, tok[:, d, :], 0.0, None, ALU.min).then_inc(*elu.at(("min", d)))
                    v.wait_ge(*eexp.after(d))
                    v.scalar_tensor_tensor(tok[:, d, :], tok[:, d, :], 0.0, e, ALU.max, ALU.add).then_inc(*elu.at(("sum", d)))
                    v.wait_ge(*elu.after(("sum", d)))
                    v.tensor_scalar(tok[:, d, :], tok[:, d, :], -1.0, None, ALU.add).then_inc(*tokr.at(("act", l.i, d)))

        eexp = sig("elu_exp")

        def elu_act(a, l):
            if l.act == "elu":
                for d in range(T):
                    a.wait_ge(*elu.after(("min", d)))
                    e = bc[0:Q, (d % 2) * D:(d % 2 + 1) * D]
                    a.activation(e, e, ACT.Exp).then_inc(*eexp.at(d))

        def x_done(l, t):
            return [agr.after((l.i, "fin", t, l.parts - 1))]

        def bias_pool(g, l, norm_i):
            if not l.last:
                return
            pool_wait(g)
            g.wait_ge(*bias_in.after(("b", l.i)))
            g.wait_ge(*tokr.after((norm_i, T - 1)))
            for t in range(T):
                g.tensor_tensor(x[:, t, :], x[:, t, :], bb[:], ALU.add).then_inc(*pool_event(bx, (l.i, t)))

        def head_rows(l, r):
            return [(r, h) for h in range(l.H)]

        def gnn_pe(pe, l):
            for e in before.get(("pe", l.i), []):
                pe.wait_ge(*e())
            if l.att is not None:
                for r in range(l.R):
                    wq_pe(pe, l, r)
            turn_pe(pe, l.turn, turn_ready[l.turn])
            if l.att is not None:
                for r in range(l.R):
                    col_pe(pe, l, r)
                for r in range(min(2, l.R)):
                    turnrow_pe(pe, ("as", l.i, r), ac[:, r, :, :], 1 + r, l, aca.after((l.i, r)))
            for r in range(l.R):
                jobs = [(t, hf) for t in range(T) for hf in range(2)]
                if r == 0 and l.R > 2:
                    lin_pe(pe, l, r, jobs[:3])
                    turnrow_pe(pe, ("as", l.i, 2), ac[:, 2, :, :], 3, l, aca.after((l.i, 2)))
                    lin_pe(pe, l, r, jobs[3:])
                else:
                    lin_pe(pe, l, r, jobs)
                if l.att is not None:
                    for w in range(2):
                        turnrow_pe(pe, ("R", w, l.i, r), Rc[:, r, w, :, :], w, l, agv.after((l.i, "R", r)))
                agg_pe(pe, l, r)

        def gnn_act(a, l):
            for e in before.get(("act", l.i), []):
                a.wait_ge(*e())
            if l.att is not None:
                for r in range(l.R):
                    wq_act(a, l, r, lambda: [tmp01_free(l)] if l.i > 0 and r == 0 else [])
            if l.att is None:
                split_act(a, l, 0)
            if l.R > 1:
                split_act(a, l, 0)
            if l.turn in turn_norm:
                norm_act(a, l.turn)
            turn_act(a, l.turn, xT_free[l.turn])
            if l.att is not None:
                for r in range(l.R):
                    col_act(a, l, r)

                def as_row(r):
                    prev = [bcg.after(("as", l.i, r - 2, l.H - 1))] if r > 1 else []
                    if r < 2 and l.i > 0:
                        p = [z for z in L[:l.i] if z.att is not None][-1]
                        prev = [bcg.after(("R2", p.i, p.R - 1, p.H - 1))]
                    turnrow_act(a, ("as", l.i, r), r % 2, l, prev)
                for r in range(min(2, l.R)):
                    as_row(r)
            for r in range(l.R):
                for t in range(T):
                    for hf in range(2):
                        lin_act(a, l, r, t, hf)
                        if (t, hf) == (1, 0) and r == 0 and l.R > 2:
                            as_row(2)
                if l.att is not None:
                    prev = [bcg.after(("as", l.i, z, l.H - 1)) for z in range(max(0, l.R - 2), l.R)] + ([bcg.after(("R2", l.i, r - 1, l.H - 1))] if r > 0 else [])
                    for w in range(2):
                        turnrow_act(a, ("R", w, l.i, r), w, l, prev)
                tiles = [(h, s) for h in range(l.H) for s in range(T)]
                for n in range(len(tiles) + 2):
                    if n < len(tiles):
                        p_act_first(a, l, r, *tiles[n])
                    if 0 < n <= len(tiles):
                        p_act_exp(a, l, r, *tiles[n - 1])
                    if n > 1:
                        p_act_high(a, l, r, *tiles[n - 2])
                    split_act(a, l, r + 1, next_weights(l, r, n))
            elu_act(a, l)

        def gnn_dve(v, l):
            for e in before.get(("dve", l.i), []):
                v.wait_ge(*e())
            if l.att is not None:
                for r in range(l.R):
                    wq_dve(v, l, r)
            if l.turn in turn_norm:
                norm_dve(v, l.turn, turn_norm[l.turn][0], turn_norm[l.turn][1])
            turn_dve(v, l.turn, xT_free[l.turn])
            if l.att is None:
                v.wait_ge(*disa.after(0))
                v.reciprocal(dis[:], dis[:]).then_inc(*agv.at("dis"))
            if l.att is not None:
                for r in range(l.R):
                    na_dve(v, l, r)
                    spread_dve(v, ("as", l.i, r), ac[:, r, :, :], 1 + r, l, [done.after(("wqp", l.i, l.R - 1, K - 1))] if r == 0 else [])
                for r in range(l.R):
                    max_dve(v, l, r)
                m_dve(v, l)
            for r in range(l.R):
                if l.att is not None:
                    free = [agv.after((l.i, "R", r))] + (prev_tile(l, r, 0, 0, pl, 1) if r > 0 else [])
                    for w in range(2):
                        spread_dve(v, ("R", w, l.i, r), Rc[:, r, w, :, :], w, l, free)
                if r > 0 or l.att is None:
                    for t in range(T):
                        for hf in range(2):
                            lin_dve(v, l, r, t, hf)
                tiles = [(h, s) for h in range(l.H) for s in range(T)]
                for n in range(len(tiles) + 1):
                    if n < len(tiles):
                        p_dve_diff(v, l, r, *tiles[n])
                    if n > 0:
                        p_dve_value(v, l, r, *tiles[n - 1])
                        if l.H > 1 and tiles[n - 1][1] == 2 and tiles[n - 1][0] > 0:
                            agg_dve(v, l, r, tiles[n - 1][0] - 1)
                agg_dve(v, l, r, l.H - 1 if l.H > 1 else None)
            fin_dve(v, l)

        disa = sig("degree_root")

        def gnn_pool(g, l, norm_i):
            for e in before.get(("pool", l.i), []):
                g.wait_ge(*e())
            ones_pool(g, l)
            split_pool(g, l, 0)
            if l.att is not None:
                for r in range(l.R):
                    g.wait_ge(*rowa.after((("as", l.i, r), 1)))
                    for h in range(l.H):
                        broadcast(g, ("as", l.i, r, h), r % 2, h, l.H)
            bias_pool(g, l, norm_i)
            for r in range(l.R):
                if l.att is not None:
                    g.wait_ge(*rowa.after((("R", 1, l.i, r), 1)))
                for h in range(l.H):
                    for z in ([0, 1] if h == 0 else [h + 1]):
                        if l.att is not None and z < l.H:
                            broadcast(g, ("R1", l.i, r, z), 0, z, l.H)
                            broadcast(g, ("R2", l.i, r, z), 1, z, l.H)
                    for s in range(T):
                        p_pool(g, l, r, h, s)
                        split_pool(g, l, r + 1, next_weights(l, r, h * T + s))
                for n in (T, T + 1):
                    if l.H == 1:
                        split_pool(g, l, r + 1, next_weights(l, r, n))

        before = {}
        turn_ready = {}
        turn_norm = {}
        xT_free = {}
        for i in (0,):
            turn_norm[0] = (lambda t: [x_in.after("x")], lambda: [done.after(("ctT", REL - 1, T - 1, 1)), vstep.after(("tot", REL - 1)), cnt.after(("mask", REL - 1))])
            turn_ready[0] = lambda t: tokr.after((0, t))
            xT_free[0] = lambda: []
        turn_ready[1] = lambda t: tokr.after(("act", 0, t))
        xT_free[1] = lambda: [done.after(("lin", 0, 0, T - 1, 1))]

        def gnn_x(i):
            return lambda t: [agr.after((i, "fin", t, L[i].parts - 1))]

        def wire(turn, x_event, tok_free, xfree):
            turn_norm[turn] = (x_event, tok_free)
            turn_ready[turn] = lambda t: tokr.after((turn, t))
            xT_free[turn] = xfree

        def lin_end(i):
            return lambda: [done.after(("lin", i, L[i].R - 1, T - 1, 1))]

        wire(2, gnn_x(1), lambda: [done.after(("turn", 1, T - 1, 1))], lin_end(1))
        wire(3, lambda t: [fv.after(("f0", "x", t))], lambda: [fv.after(("f0", "x", T - 1))], lambda: [done.after(("f0", "h", 1))])
        turn_ready[4] = lambda t: tokr.after(("act", 2, t))
        xT_free[4] = lin_end(2)
        wire(5, gnn_x(3), lambda: [done.after(("turn", 4, T - 1, 1))], lin_end(3))
        wire(6, lambda t: [fv.after(("f1", "x", t))], lambda: [fv.after(("f1", "x", T - 1))],
             lambda: [done.after(("f1", "z", NE * NCH - 1, 1, 1))])
        wire(7, gnn_x(4), lambda: [done.after(("turn", 6, T - 1, 1))], lin_end(4))
        wire(8, lambda t: [fv.after(("f2", "x", NE - 1, t, 1))], lambda: [done.after(("turn", 7, T - 1, 1))],
             lambda: [done.after(("f2", "h", NE - 1, 1))])
        turn_ready[9] = lambda t: tokr.after(("act", 5, t))
        xT_free[9] = lin_end(5)
        wire(10, gnn_x(6), lambda: [agr.after((6, "fin", T - 1, 1))], lin_end(6))

        def gnn_end(i, signal):
            return signal.after((i, L[i].R - 1, L[i].H - 1, T - 1))

        f0g = tmp[0:F0, 0:NP]
        f0q = tmp[0:F0, 640:640 + NP // 2].bitcast(BF16)
        f0w2 = tmp[0:F0, 960:960 + D // 2].bitcast(BF16)

        def f0_sp(sp):
            load_raw(sp, ("f0", "w1"), [(lambda v: v[0:F0, 0, :], I["L0_ffn_W1"])])
            load_raw(sp, ("f0", "w2"), [(lambda v: v[:, 0, 0:K * F0].rearrange("p (j h) -> p j h", h=F0),
                                         I["L0_ffn_W2"].rearrange("(j p) h -> p j h", p=128))])
            load_bias(sp, ("f0", "bias"), "L0_ffn_b2")

        def f0_quant_dve(v):
            w1, w2 = raw(("f0", "w1"))[0:F0, 0, :], raw(("f0", "w2"))[:, 0, 0:K * F0]
            wait_raw(v, ("f0", "w1"))
            v.tensor_reduce(sm[0:F0, 2:3], w1, AX.X, ALU.max, apply_absolute_value=True).then_inc(*fv.at(("f0", "max1")))
            wait_raw(v, ("f0", "w2"))
            v.tensor_reduce(sm[:, 3:4], w2, AX.X, ALU.max, apply_absolute_value=True).then_inc(*fv.at(("f0", "max2")))
            v.wait_ge(*par.after("all"))
            v.reciprocal(sm[:, 6:8], sm[:, 0:2]).then_inc(*fv.at(("f0", "inv")))
            for n, (w, P_) in enumerate(((w1, F0), (w2, 128))):
                v.wait_ge(*fg.after(("f0", "max", n)))
                v.tensor_scalar(sm[0:P_, 4 + n:5 + n], sm[0:P_, 4 + n:5 + n], 1.0 / 127.0, None, ALU.mult).then_inc(*fv.at(("f0", "s", n)))
                v.wait_ge(*fv.after(("f0", "s", n)))
                v.reciprocal(sm[0:P_, 8 + n:9 + n], sm[0:P_, 4 + n:5 + n]).then_inc(*fv.at(("f0", "r", n)))
                v.wait_ge(*fv.after(("f0", "r", n)))
                v.tensor_scalar(w, w, sm[0:P_, 8 + n:9 + n], MAGIC, ALU.mult, ALU.add).then_inc(*fv.at(("f0", "q", n)))
                v.wait_ge(*fv.after(("f0", "q", n)))
                v.tensor_scalar(w, w, MAGIC, 127.0, ALU.subtract, ALU.min).then_inc(*fv.at(("f0", "w", n)))
            v.tensor_tensor(sm[:, 10:11], sm[:, 5:6], sm[:, 0:1], ALU.mult).then_inc(*fv.at(("f0", "s2")))

        def f0_max_pool(g):
            pool_wait(g)
            g.wait_ge(*fv.after(("f0", "max1")))
            g.partition_all_reduce(sm[0:F0, 4:5], sm[0:F0, 2:3], F0, RMAX).then_inc(*pool_event(fg, ("f0", "max", 0)))
            pool_wait(g)
            g.wait_ge(*fv.after(("f0", "max2")))
            g.partition_all_reduce(sm[:, 5:6], sm[:, 3:4], 128, RMAX).then_inc(*pool_event(fg, ("f0", "max", 1)))

        def f0_pe(pe):
            w1, w2 = raw(("f0", "w1"))[0:F0, 0, :], raw(("f0", "w2"))[:, 0, 0:K * F0]
            for b in range(2):
                ps = open_job(pe, ("f0", "t1", b))
                pe.wait_ge(*fv.after(("f0", "w", 0)))
                for j in range(3):
                    k = 3 * b + j
                    m = pe.transpose(ps[:, j * F0:(j + 1) * F0], w1[:, k * 128:(k + 1) * 128], ident[0:F0, 0:F0])
                m.then_inc(*(raw_reader(("f0", "w1"), done, ("f0", "t1", b)) if b else done.at(("f0", "t1", b))))
            for b in range(2):
                ps = open_job(pe, ("f0", "t2", b))
                pe.wait_ge(*fv.after(("f0", "w", 1)))
                for j in range(3):
                    k = 3 * b + j
                    m = pe.transpose(ps[0:F0, j * 128:(j + 1) * 128], w2[:, k * F0:(k + 1) * F0], ident[:, :])
                m.then_inc(*(raw_reader(("f0", "w2"), done, ("f0", "t2", b)) if b else done.at(("f0", "t2", b))))
            turn_pe(pe, 2, turn_ready[2])
            pe.wait_ge(*xT_whole(2))
            for c, (c0, w) in enumerate(HALF):
                ps = open_job(pe, ("f0", "h", c))
                if c == 0:
                    pe.wait_ge(*fa.after(("f0", "w1", 1)))
                for k in range(K):
                    for n, xt in enumerate((xTh, xTl)):
                        m = pe.matmul(ps[0:F0, 0:w], Wh[:, k * F0:(k + 1) * F0], xt[:, k, c0:c0 + w],
                                      start=k == 0 and n == 0, stop=k == K - 1 and n == 1)
                m.then_inc(*done.at(("f0", "h", c)))
            for t in range(T):
                for hf in range(2):
                    ps = open_job(pe, ("f0", "o", t, hf))
                    pe.wait_ge(*fv.after(("f0", "hq", 1)))
                    pe.matmul(ps[0:Q, 0:HD], f0q[:, t * Q:(t + 1) * Q], f0w2[:, hf * HD:(hf + 1) * HD],
                              start=True, stop=True).then_inc(*done.at(("f0", "o", t, hf)))

        def f0_act(a):
            a.wait_ge(*gnn_end(1, pl))
            for b in range(2):
                a.wait_ge(*done.after(("f0", "t1", b)))
                a.activation(Wh[:, b * 3 * F0:(b + 1) * 3 * F0], bank(("f0", "t1", b))[:, 0:3 * F0], ACT.Copy).then_inc(
                    *frees(("f0", "t1", b), fa, ("f0", "w1", b)))
            for b in range(2):
                a.wait_ge(*done.after(("f0", "t2", b)))
                a.activation(f0w2[:, b * HD:(b + 1) * HD], bank(("f0", "t2", b))[0:F0, 0:HD], ACT.Copy).then_inc(
                    *frees(("f0", "t2", b), fa, ("f0", "w2", b)))
            norm_act(a, 2)
            turn_act(a, 2, xT_free[2])
            a.wait_ge(*fv.after(("f0", "s", 0)))
            for c, (c0, w) in enumerate(HALF):
                a.wait_ge(*done.after(("f0", "h", c)))
                a.activation(f0g[:, c0:c0 + w], bank(("f0", "h", c))[0:F0, 0:w], ACT.Gelu, bias=b1c[0:F0, 3:4],
                             scale=sm[0:F0, 4:5]).then_inc(*frees(("f0", "h", c), fa, ("f0", "g", c)))

        def f0_dve(v):
            f0_quant_dve(v)
            norm_dve(v, 2, *turn_norm[2])
            turn_dve(v, 2, xT_free[2])
            for c, (c0, w) in enumerate(HALF):
                g_ = f0g[:, c0:c0 + w]
                v.wait_ge(*fa.after(("f0", "g", c)))
                v.tensor_scalar(g_, g_, sm[0:F0, 6:7], MAGIC, ALU.mult, ALU.add).then_inc(*fv.at(("f0", "g1", c)))
                v.wait_ge(*fv.after(("f0", "g1", c)))
                v.tensor_scalar(g_, g_, MAGIC + 127.0, MAGIC - 128.0, ALU.min, ALU.max).then_inc(*fv.at(("f0", "g2", c)))
                v.wait_ge(*fv.after(("f0", "g2", c)))
                v.tensor_scalar(f0q[:, c0:c0 + w], g_, MAGIC, None, ALU.subtract).then_inc(*fv.at(("f0", "hq", c)))
            v.wait_ge(*fv.after(("f0", "s2")))
            v.wait_ge(*bias_in.after(("f0", "bias")))
            for t in range(T):
                for hf in range(2):
                    y = tok[:, t, hf * HD:(hf + 1) * HD]
                    v.wait_ge(*done.after(("f0", "o", t, hf)))
                    m = v.scalar_tensor_tensor(y, bank(("f0", "o", t, hf))[0:Q, 0:HD], sm[0:Q, 10:11],
                                               bb[:, hf * HD:(hf + 1) * HD], ALU.mult, ALU.add)
                    last = t == T - 1 and hf == 1
                    m.then_inc(*frees(("f0", "o", t, hf), fv, ("f0", "bias") if last else ("f0", "y", t, hf)))
            v.wait_ge(*fv.after(("f0", "bias")))
            for t in range(T):
                v.tensor_scalar(tok[:, t, :], tok[:, t, :], sm[0:Q, 7:8], MAGIC, ALU.mult, ALU.add).then_inc(*fv.at(("f0", "y1", t)))
            for t in range(T):
                v.wait_ge(*fv.after(("f0", "y1", t)))
                v.tensor_scalar(tok[:, t, :], tok[:, t, :], MAGIC + 127.0, MAGIC - 128.0, ALU.min, ALU.max).then_inc(*fv.at(("f0", "y2", t)))
            for t in range(T):
                v.wait_ge(*fv.after(("f0", "y2", t)))
                v.tensor_scalar(tok[:, t, :], tok[:, t, :], MAGIC, sm[0:Q, 1:2], ALU.subtract, ALU.mult).then_inc(*fv.at(("f0", "y3", t)))
            for t in range(T):
                v.wait_ge(*fv.after(("f0", "y3", t)))
                v.tensor_tensor(x[:, t, :], x[:, t, :], tok[:, t, :], ALU.add).then_inc(*fv.at(("f0", "x", t)))

        def f0_pool(g):
            f0_max_pool(g)

        before["act", 2] = [lambda: fv.after(("f0", "hq", 1)), lambda: done.after(("f0", "o", T - 1, 1))]

        def r8(i):
            return Rc[:].rearrange("p r w t h -> p (r w t h)")[:, i * 8 * T:(i + 1) * 8 * T].rearrange("p (t e) -> p t e", e=8)
        iota8 = dn[:].rearrange("p t h -> p (t h)")[:, 0:8]
        ri = st[:].rearrange("p t a b -> p (t a b)")[:, 0:8 * T].bitcast(U32).rearrange("p (t e) -> p t e", e=8)
        weight = rt[:, :, 16:24]

        def route_dve(v, i, eps):
            n = [0]

            def step(m, *key):
                m.then_inc(*fv.at((i, "route") + (key or (n[0],))))
                v.wait_ge(*fv.after((i, "route") + (key or (n[0],))))
                n[0] += 1
            lg, pr, m8 = rt[:, :, 0:8], rt[:, :, 8:16], r8(2)
            wide = lambda c: c.to_broadcast([Q, T, 8])
            step(v.tensor_reduce(sd[:], lg, AX.X, ALU.max))
            step(v.tensor_tensor(lg, lg, wide(sd[:].unsqueeze(2)), ALU.subtract), "z")
            v.wait_ge(*fa.after((i, "exp")))
            step(v.tensor_reduce(sd[:], pr, AX.X, ALU.add))
            step(v.reciprocal(rs[:], sd[:]))
            step(v.tensor_tensor(pr, pr, wide(rs[:].unsqueeze(2)), ALU.mult))
            for t in range(T):
                step(v.max(m8[:, t, :], pr[:, t, :]))
                step(v.max_index(ri[:, t, :], m8[:, t, :], pr[:, t, :]))
            step(v.tensor_copy(mt[:, :, 0:2], ri[:, :, 0:2]))
            step(v.tensor_tensor(sd[:], m8[:, :, 0], m8[:, :, 1], ALU.add))
            if eps:
                step(v.tensor_scalar(sd[:], sd[:], eps, None, ALU.add))
            step(v.reciprocal(rs[:], sd[:]))
            step(v.tensor_tensor(mm[:, :, 0:2], m8[:, :, 0:2], rs[:].unsqueeze(2).to_broadcast([Q, T, 2]), ALU.mult))
            io = iota8.unsqueeze(1).to_broadcast([Q, T, 8])
            for c in range(2):
                step(v.tensor_tensor(r8(c), io, wide(mt[:, :, c:c + 1]), ALU.is_equal))
                step(v.tensor_tensor(r8(c), r8(c), wide(mm[:, :, c:c + 1]), ALU.mult))
            v.tensor_tensor(weight, r8(0), r8(1), ALU.add).then_inc(*fv.at((i, "weight")))

        def route_act(a, i):
            a.wait_ge(*fv.after((i, "route", "z")))
            a.activation(rt[:, :, 8:16], rt[:, :, 0:8], ACT.Exp).then_inc(*fa.at((i, "exp")))

        NC = NE * NCH
        f1w2 = bc[:, 1300:1324].rearrange("p (m e) -> p m e", e=8)
        f1b2 = bc[0:Q, 1330:1338]
        beta = rows[0:Q, 0:D]

        def wslot(n):
            return (Wh, Wl) if n % 2 == 0 else (Ph, Pl)

        def zf(n):
            return (tmp if n % 2 == 0 else bc)[:, 0:2 * NP].rearrange("p (d c) -> p d c", c=NP)

        def zs(buf, n):
            return buf[:, (n % 2) * 2 * NP:(n % 2 + 1) * 2 * NP].rearrange("p (d c) -> p d c", c=NP)

        def f1_sp(sp):
            load_raw(sp, ("f1", "w1"), [(lambda v: v.rearrange("p a b -> p (a b)")[:, 0:K * RW].rearrange("p (k m) -> p k m", m=RW),
                                         I["L1_ffn_w1"].rearrange("(k p) m -> p k m", p=128))], 3)
            sp.wait_ge(*gnn_end(3, pn2))
            sp.wait_ge(*agv.after((3, "n1", 0, 0, T - 1)))
            sp.dma_start(f1w2, I["L1_ffn_w2"].rearrange("(m p) e -> p m e", p=128)).then_inc(*fd.at("f1", 16))
            sp.dma_start(f1b2, I["L1_ffn_b2"].partition_broadcast(Q)).then_inc(*fd.at("f1", 16))
            sp.wait_ge(*bcg.after(("R2", 3, 0, 0)))
            sp.dma_start(beta, I["L1_ffn_beta"].partition_broadcast(Q)).then_inc(*fd.at("f1", 16))
            load_bias(sp, ("f1", "gamma"), "L1_ffn_gamma")
            for n in range(NC):
                e, c = divmod(n, NCH)
                load_raw(sp, ("f1", "d", n), [(lambda v: v.rearrange("p a b -> p (a b)").rearrange("p (k m) -> p k m", m=CW),
                                               I["L1_ffn_down_w"][e].rearrange("(k p) f -> p k f", p=128)[:, :, c * CW:(c + 1) * CW])], 2)
                load_raw(sp, ("f1", "u", n), [(lambda v: v, I["L1_ffn_up_w"][e, c * CW:(c + 1) * CW, :].rearrange("(d p) h -> p d h", p=128))], 2)

        def flat(v):
            return v.rearrange("p a b -> p (a b)")

        def f1_split_act(a, n):
            wh = wslot(n)[0]
            for i, part in enumerate("du"):
                wait_raw(a, ("f1", part, n))
                if n == 0 and i == 0:
                    a.wait_ge(*done.after(("f1", "r", 2, 1)))
                elif n == 1 and i == 0:
                    a.wait_ge(*agg_end(L[3], 0))
                elif n >= 2:
                    a.wait_ge(*done.after(("f1", "z", n - 2, 1, 1) if i == 0 else ("f1", "u", n - 2, T - 1, 1)))
                a.activation(wh[:, i * 2 * D:(i + 1) * 2 * D], flat(raw(("f1", part, n), 2)), ACT.Copy).then_inc(
                    *raw_reader(("f1", part, n), whi, ("f1", part, n)))

        def f1_split_pool(g, n):
            wh, wl = wslot(n)
            if n == 0:
                pool_wait(g)
            for i, part in enumerate("du"):
                g.wait_ge(*whi.after(("f1", part, n)))
                g.tensor_tensor(wl[:, i * 2 * D:(i + 1) * 2 * D], flat(raw(("f1", part, n), 2)),
                                wh[:, i * 2 * D:(i + 1) * 2 * D].bitcast(F32), ALU.subtract).then_inc(
                    *pool_event(wlo, ("f1", part, n), raw_reader(("f1", part, n), wlo, ("f1", part, n))))

        def f1_z_pe(pe, n):
            wh, wl = wslot(n)
            pe.wait_ge(*wlo.after(("f1", "d", n)))
            for d in range(2):
                for c, (c0, w) in enumerate(HALF):
                    ps = open_job(pe, ("f1", "z", n, d, c))
                    for k in range(K):
                        for i, (s_, m_) in enumerate(pairs((wh, xTh), (wl, xTl))):
                            m = pe.matmul(ps[:, 0:w], s_[:, k * CW + d * 128:k * CW + (d + 1) * 128], m_[:, k, c0:c0 + w],
                                          start=k == 0 and i == 0, stop=k == K - 1 and i == 2)
                    m.then_inc(*done.at(("f1", "z", n, d, c)))

        def f1_u_pe(pe, n):
            pe.wait_ge(*wlo.after(("f1", "u", n)))
            pe.wait_ge(*fv.after(("f1", "zl", n, 1)))
            zh, zl = zs(hh, n), zs(hl, n)
            wh, wl = wslot(n)
            for t in range(T):
                for hf in range(2):
                    ps = open_job(pe, ("f1", "u", n, t, hf))
                    for d in range(2):
                        for i, (s_, m_) in enumerate(pairs((zh, wh), (zl, wl))):
                            c = 2 * D + d * D + hf * HD
                            m = pe.matmul(ps[0:Q, 0:HD], s_[:, d, t * Q:(t + 1) * Q], m_[:, c:c + HD],
                                          start=d == 0 and i == 0, stop=d == 1 and i == 2)
                    m.then_inc(*done.at(("f1", "u", n, t, hf)))

        def f1_z_act(a, n):
            e, c_ = divmod(n, NCH)
            z = zf(n)
            if n == 0:
                a.wait_ge(*done.after(("f1", "logits")))
            if n == 1:
                a.wait_ge(*fv.after(("f1", "logits")))
            if n >= 2:
                a.wait_ge(*fv.after(("f1", "zl", n - 2, 1)))
            for d in range(2):
                for c, (c0, w) in enumerate(HALF):
                    a.wait_ge(*done.after(("f1", "z", n, d, c)))
                    a.activation(z[:, d, c0:c0 + w], bank(("f1", "z", n, d, c))[:, 0:w], ACT.Gelu,
                                 bias=gb[:, n * 2 + d:n * 2 + d + 1]).then_inc(*frees(("f1", "z", n, d, c), fa, ("f1", "g", n, d, c)))
                a.wait_ge(*fa.after(("f1", "g", n, d, 1)))
                if d == 0 and n >= 2:
                    a.wait_ge(*done.after(("f1", "u", n - 2, T - 1, 1)))
                a.activation(zs(hh, n)[:, d, :], z[:, d, :], ACT.Copy).then_inc(*fa.at(("f1", "zh", n, d)))

        def f1_z_dve(v, n):
            for d in range(2):
                v.wait_ge(*fa.after(("f1", "zh", n, d)))
                v.tensor_tensor(zs(hl, n)[:, d, :], zf(n)[:, d, :], zs(hh, n)[:, d, :].bitcast(F32),
                                ALU.subtract).then_inc(*fv.at(("f1", "zl", n, d)))

        def f1_u_dve(v, n):
            e = n // NCH
            for t in range(T):
                for hf in range(2):
                    y = tok[:, t, hf * HD:(hf + 1) * HD]
                    v.wait_ge(*done.after(("f1", "u", n, t, hf)))
                    if n > 0:
                        v.wait_ge(*fv.after(("f1", "y", n - 1, t, hf)))
                    v.scalar_tensor_tensor(y, bank(("f1", "u", n, t, hf))[0:Q, 0:HD], weight[:, t, e:e + 1], y,
                                           ALU.mult, ALU.add).then_inc(*frees(("f1", "u", n, t, hf), fv, ("f1", "y", n, t, hf)))

        def f1_pe(pe):
            turn_pe(pe, 5, turn_ready[5])
            pe.wait_ge(*xT_whole(5))
            for m_i in range(3):
                for c, (c0, w) in enumerate(HALF):
                    ps = open_job(pe, ("f1", "r", m_i, c))
                    if m_i == 0 and c == 0:
                        pe.wait_ge(*fg.after(("f1", "w1")))
                    for k in range(K):
                        for i, (s_, x_) in enumerate(pairs((Wh, xTh), (Wl, xTl))):
                            m = pe.matmul(ps[:, 0:w], s_[:, k * RW + m_i * 128:k * RW + (m_i + 1) * 128], x_[:, k, c0:c0 + w],
                                          start=k == 0 and i == 0, stop=k == K - 1 and i == 2)
                    m.then_inc(*done.at(("f1", "r", m_i, c)))
            ps = open_job(pe, ("f1", "logits"))
            pe.wait_ge(*fd.after("f1"))
            pe.wait_ge(*fa.after(("f1", "rg", 2, 1)))
            for t in range(T):
                for m_i in range(3):
                    m = pe.matmul(ps[0:Q, t * 8:(t + 1) * 8], tmp[:, m_i * NP + t * Q:m_i * NP + (t + 1) * Q], f1w2[:, m_i, :],
                                  start=m_i == 0, stop=m_i == 2)
            m.then_inc(*done.at(("f1", "logits")))
            f1_z_pe(pe, 0)
            for n in range(NC):
                if n + 1 < NC:
                    f1_z_pe(pe, n + 1)
                f1_u_pe(pe, n)

        def f1_act(a):
            wait_raw(a, ("f1", "w1"))
            a.wait_ge(*done.after(("lin", 3, 0, T - 1, 1)))
            a.activation(Wh[:, 0:K * RW], flat(raw(("f1", "w1"), 3)), ACT.Copy).then_inc(
                *raw_reader(("f1", "w1"), fa, ("f1", "w1")))
            norm_act(a, 5)
            turn_act(a, 5, xT_free[5])
            a.wait_ge(*gnn_end(3, pl))
            for m_i in range(3):
                for c, (c0, w) in enumerate(HALF):
                    a.wait_ge(*done.after(("f1", "r", m_i, c)))
                    a.activation(tmp[:, m_i * NP + c0:m_i * NP + c0 + w], bank(("f1", "r", m_i, c))[:, 0:w], ACT.Gelu,
                                 bias=b1c[:, m_i:m_i + 1]).then_inc(*frees(("f1", "r", m_i, c), fa, ("f1", "rg", m_i, c)))
            f1_split_act(a, 0)
            route_act(a, "f1")
            f1_split_act(a, 1)
            f1_z_act(a, 0)
            for n in range(NC):
                if n + 1 < NC:
                    f1_z_act(a, n + 1)
                if n + 2 < NC:
                    f1_split_act(a, n + 2)
            norm_act(a, "f1")

        def f1_dve(v):
            norm_dve(v, 5, *turn_norm[5])
            turn_dve(v, 5, xT_free[5])
            v.wait_ge(*consts.after("iota8"))
            v.tensor_copy(iota8, dn8[:]).then_inc(*fv.at(("f1", "iota")))
            v.wait_ge(*done.after(("f1", "logits")))
            for t in range(T):
                v.tensor_tensor(rt[:, t, 0:8], bank(("f1", "logits"))[0:Q, t * 8:(t + 1) * 8], f1b2, ALU.add).then_inc(
                    *(frees(("f1", "logits"), fv, ("f1", "logits")) if t == T - 1 else fv.at(("f1", "lg", t))))
            v.wait_ge(*fv.after(("f1", "logits")))
            route_dve(v, "f1", 1e-8)
            v.wait_ge(*fv.after(("f1", "weight")))
            f1_z_dve(v, 0)
            for n in range(NC):
                if n + 1 < NC:
                    f1_z_dve(v, n + 1)
                f1_u_dve(v, n)
            norm_dve(v, "f1", lambda t: [fv.after(("f1", "y", NC - 1, t, 1))], lambda: [], src=tok, dst=tok)
            v.wait_ge(*bias_in.after(("f1", "gamma")))
            for t in range(T):
                v.wait_ge(*tokr.after(("f1", t)))
                v.tensor_tensor(tok[:, t, :], tok[:, t, :], bb[:], ALU.mult).then_inc(
                    *fv.at(("f1", "gamma") if t == T - 1 else ("f1", "gm", t)))
            for t in range(T):
                v.wait_ge(*fv.after(("f1", "gamma") if t == T - 1 else ("f1", "gm", t)))
                v.wait_ge(*fg.after(("f1", "beta", t)))
                v.tensor_tensor(x[:, t, :], x[:, t, :], tok[:, t, :], ALU.add).then_inc(*fv.at(("f1", "x", t)))

        def f1_pool(g):
            pool_wait(g)
            g.wait_ge(*fa.after(("f1", "w1")))
            g.tensor_tensor(Wl[:, 0:K * RW], flat(raw(("f1", "w1"), 3)), Wh[:, 0:K * RW].bitcast(F32), ALU.subtract).then_inc(
                *pool_event(fg, ("f1", "w1"), raw_reader(("f1", "w1"), fg, ("f1", "w1"))))
            f1_split_pool(g, 0)
            f1_split_pool(g, 1)
            g.wait_ge(*fd.after("f1"))
            g.wait_ge(*tokr.after((5, T - 1)))
            for t in range(T):
                g.tensor_tensor(x[:, t, :], x[:, t, :], beta, ALU.add).then_inc(*pool_event(fg, ("f1", "beta", t)))
            for n in range(2, NC):
                f1_split_pool(g, n)

        W2W = K * F0 + D

        def f2_sp(sp):
            load_raw(sp, ("f2", "r"), [(lambda v: v[0:NE, 0, :], I["L2_ffn_router_w"])])
            for e in range(NE):
                load_raw(sp, ("f2", e), [
                    (lambda v: v[:, 0, 0:K * F0].rearrange("p (k m) -> p k m", m=F0), I["L2_ffn_w1"][e].rearrange("(k p) m -> p k m", p=128)),
                    (lambda v: v[0:F0, 1, :], I["L2_ffn_w2"][e]),
                    (lambda v: v[F0:F0 + 1, 1, :], I["L2_ffn_b2"][e:e + 1, :])], 2)

        def f2w(buf, e):
            b = (e % 2) * W2W
            return buf[:, b:b + K * F0], buf[0:F0 + 1, b + K * F0:b + W2W]

        def f2h(buf, e):
            return buf[:, (e % 2) * NP:(e % 2 + 1) * NP]

        def f2f(e):
            return (tmp if e % 2 == 0 else bc)[0:F0, 0:NP]

        def f2_split_act(a, e):
            wait_raw(a, ("f2", e))
            if e < 2:
                a.wait_ge(*done.after(("lin", 4, 0, T - 1, 1)))
            else:
                a.wait_ge(*done.after(("f2", "o", e - 2, T - 1, 1)))
            w1, w2 = f2w(Wh, e)
            r_ = raw(("f2", e), 2)
            a.activation(w1, r_[:, 0, 0:K * F0], ACT.Copy).then_inc(*fa.at(("f2", "w1", e)))
            a.activation(w2, r_[0:F0 + 1, 1, :], ACT.Copy).then_inc(*raw_reader(("f2", e), fa, ("f2", "w2", e)))

        def f2_split_pool(g, e):
            g.wait_ge(*fa.after(("f2", "w2", e)))
            if e == 0:
                pool_wait(g)
            for i, (h_, l_) in enumerate(zip(f2w(Wh, e), f2w(Wl, e))):
                r_ = raw(("f2", e), 2)
                src = r_[:, 0, 0:K * F0] if i == 0 else r_[0:F0 + 1, 1, :]
                m = g.tensor_tensor(l_, src, h_.bitcast(F32), ALU.subtract)
            m.then_inc(*pool_event(fg, ("f2", e), raw_reader(("f2", e), fg, ("f2", e))))

        def f2_h_pe(pe, e):
            pe.wait_ge(*fg.after(("f2", e)))
            for c, (c0, w) in enumerate(HALF):
                ps = open_job(pe, ("f2", "h", e, c))
                for k in range(K):
                    for i, (s_, x_) in enumerate(pairs((f2w(Wh, e)[0], xTh), (f2w(Wl, e)[0], xTl))):
                        m = pe.matmul(ps[0:F0, 0:w], s_[:, k * F0:(k + 1) * F0], x_[:, k, c0:c0 + w],
                                      start=k == 0 and i == 0, stop=k == K - 1 and i == 2)
                m.then_inc(*done.at(("f2", "h", e, c)))

        def f2_o_pe(pe, e):
            pe.wait_ge(*fv.after(("f2", "hl", e)))
            if e == 0:
                pe.wait_ge(*fg.after(("f2", "ones")))
            for t in range(T):
                for hf in range(2):
                    ps = open_job(pe, ("f2", "o", e, t, hf))
                    for i, (s_, m_) in enumerate(pairs((f2h(hh, e), f2w(Wh, e)[1]), (f2h(hl, e), f2w(Wl, e)[1]))):
                        m = pe.matmul(ps[0:Q, 0:HD], s_[0:F0 + 1, t * Q:(t + 1) * Q], m_[:, hf * HD:(hf + 1) * HD],
                                      start=i == 0, stop=i == 2)
                    m.then_inc(*done.at(("f2", "o", e, t, hf)))

        def f2_pe(pe):
            ps = open_job(pe, ("f2", "rT"))
            wait_raw(pe, ("f2", "r"))
            for k in range(K):
                m = pe.transpose(ps[:, k * 8:(k + 1) * 8], raw(("f2", "r"))[0:NE, 0, k * 128:(k + 1) * 128], ident[0:NE, 0:NE])
            m.then_inc(*raw_reader(("f2", "r"), done, ("f2", "rT")))
            turn_pe(pe, 7, turn_ready[7])
            pe.wait_ge(*xT_whole(7))
            ps = open_job(pe, ("f2", "logits"))
            pe.wait_ge(*fv.after(("f2", "rl")))
            for t in range(T):
                for k in range(K):
                    for i, (s_, m_) in enumerate(pairs((xTh, Wqh), (xTl, Wql))):
                        m = pe.matmul(ps[0:Q, t * 8:(t + 1) * 8], s_[:, k, t * Q:(t + 1) * Q], m_[:, 0, k, :],
                                      start=k == 0 and i == 0, stop=k == K - 1 and i == 2)
            m.then_inc(*done.at(("f2", "logits")))
            f2_h_pe(pe, 0)
            for e in range(NE):
                if e + 1 < NE:
                    f2_h_pe(pe, e + 1)
                f2_o_pe(pe, e)

        def f2_act(a):
            a.wait_ge(*done.after(("f2", "rT")))
            a.activation(Wqh[:, 0, :, :], bank(("f2", "rT"))[:, 0:48].rearrange("p (k c) -> p k c", c=8), ACT.Copy).then_inc(*fa.at(("f2", "rh")))
            f2_split_act(a, 0)
            f2_split_act(a, 1)
            norm_act(a, 7)
            turn_act(a, 7, xT_free[7])
            route_act(a, "f2")
            for e in range(NE):
                if e >= 2:
                    a.wait_ge(*fv.after(("f2", "hl", e - 2)))
                for c, (c0, w) in enumerate(HALF):
                    a.wait_ge(*done.after(("f2", "h", e, c)))
                    a.activation(f2f(e)[:, c0:c0 + w], bank(("f2", "h", e, c))[0:F0, 0:w], ACT.Gelu,
                                 bias=b2c[0:F0, e:e + 1]).then_inc(*frees(("f2", "h", e, c), fa, ("f2", "g", e, c)))
                a.wait_ge(*fa.after(("f2", "g", e, 1)))
                if e >= 2:
                    a.wait_ge(*done.after(("f2", "o", e - 2, T - 1, 1)))
                a.activation(f2h(hh, e)[0:F0, :], f2f(e), ACT.Copy).then_inc(*fa.at(("f2", "hh", e)))
                if e >= 1 and e + 1 < NE:
                    f2_split_act(a, e + 1)

        def f2_dve(v):
            v.wait_ge(*fa.after(("f2", "rh")))
            v.tensor_tensor(Wql[:, 0, :, :], bank(("f2", "rT"))[:, 0:48].rearrange("p (k c) -> p k c", c=8),
                            Wqh[:, 0, :, :].bitcast(F32), ALU.subtract).then_inc(*frees(("f2", "rT"), fv, ("f2", "rl")))
            norm_dve(v, 7, *turn_norm[7])
            turn_dve(v, 7, xT_free[7])
            v.wait_ge(*done.after(("f2", "logits")))
            v.tensor_copy(rt[:, :, 0:8], bank(("f2", "logits"))[0:Q, 0:8 * T].rearrange("p (t e) -> p t e", e=8)).then_inc(
                *frees(("f2", "logits"), fv, ("f2", "logits")))
            v.wait_ge(*fv.after(("f2", "logits")))
            route_dve(v, "f2", 0.0)
            v.wait_ge(*fv.after(("f2", "weight")))

            def low(e):
                v.wait_ge(*fa.after(("f2", "hh", e)))
                v.tensor_tensor(f2h(hl, e)[0:F0, :], f2f(e), f2h(hh, e)[0:F0, :].bitcast(F32), ALU.subtract).then_inc(*fv.at(("f2", "hl", e)))
            low(0)
            for e in range(NE):
                if e + 1 < NE:
                    low(e + 1)
                for t in range(T):
                    for hf in range(2):
                        y = x[:, t, hf * HD:(hf + 1) * HD]
                        v.wait_ge(*done.after(("f2", "o", e, t, hf)))
                        if e > 0:
                            v.wait_ge(*fv.after(("f2", "x", e - 1, t, hf)))
                        v.scalar_tensor_tensor(y, bank(("f2", "o", e, t, hf))[0:Q, 0:HD], weight[:, t, e:e + 1], y,
                                               ALU.mult, ALU.add).then_inc(*frees(("f2", "o", e, t, hf), fv, ("f2", "x", e, t, hf)))

        def f2_pool(g):
            pool_wait(g)
            g.wait_ge(*agg_end(L[4], 0))
            g.memset(hh[F0:F0 + 1, 0:2 * NP].bitcast(F32), 1.0)
            g.memset(hl[F0:F0 + 1, 0:2 * NP].bitcast(F32), 0.0).then_inc(*pool_event(fg, ("f2", "ones")))
            for e in range(NE):
                f2_split_pool(g, e)

        h_last[5] = [lambda: done.after(("f2", "o", NE - 1, T - 1, 1))]
        before["act", 5] = [lambda: fv.after(("f2", "hl", NE - 1)), lambda: done.after(("f2", "o", NE - 1, T - 1, 1))]
        before["act", 4] = [lambda: fv.after(("f1", "zl", NC - 1, 1)), lambda: done.after(("f1", "u", NC - 1, T - 1, 1))]
        before["pool", 4] = [lambda: done.after(("f1", "u", NC - 1, T - 1, 1))]
        before["pool", 5] = [lambda: fv.after(("f2", "hl", NE - 1)), lambda: done.after(("f2", "o", NE - 1, T - 1, 1))]

        xq = tmp[:, 0:K * NP // 2].bitcast(BF16).rearrange("p (k n) -> p k n", n=NP)
        f3wi = bc[:, 0:384].bitcast(BF16)
        f3wo = bc[0:F3, 384:768].bitcast(BF16)
        f3go = bc[0:Q, 768:832]
        yq = bc[0:F3, 896:1209].bitcast(BF16)
        yy = rows[0:Q, 0:T * F3].rearrange("p (t c) -> p t c", c=F3)
        gt = rows[0:Q, T * F3:2 * T * F3].rearrange("p (t c) -> p t c", c=F3)
        junk = Wraw[0:Q, 3, :]

        def f3_sp(sp):
            load_raw(sp, ("f3", "wi"), [(lambda v: v[:, 0, :], I["L3_ffn_w_in"])])
            load_raw(sp, ("f3", "wo"), [(lambda v: v[:, 0, 0:K * F3].rearrange("p (j h) -> p j h", h=F3),
                                         I["L3_ffn_w_out"].rearrange("(j p) h -> p j h", p=128))])
            load_bias(sp, ("f3", "g"), "L3_ffn_g_in")
            sp.wait_ge(*gnn_end(6, pn2))
            sp.wait_ge(*agv.after((6, "n1", REL - 1, 0, T - 1)))
            sp.dma_start(f3go, I["L3_ffn_g_out"].partition_broadcast(Q)).then_inc(*fd.at("f3", 16))

        def f3_quant_dve(v):
            ws = (raw(("f3", "wi"))[:, 0, :], raw(("f3", "wo"))[:, 0, 0:K * F3])
            for n, w in enumerate(ws):
                wait_raw(v, ("f3", ("wi", "wo")[n]))
                v.tensor_reduce(sm[:, 2 + n:3 + n], w, AX.X, ALU.add, apply_absolute_value=True).then_inc(*fv.at(("f3", "sum", n)))
            for n, w in enumerate(ws):
                v.wait_ge(*fg.after(("f3", "sum", n)))
                c = sm[:, 4 + n:5 + n]
                v.tensor_scalar(c, c, 1.0 / (128 * w.shape[1]), 1e-5, ALU.mult, ALU.max).then_inc(*fv.at(("f3", "s", n)))
                v.wait_ge(*fv.after(("f3", "s", n)))
                v.reciprocal(sm[:, 8 + n:9 + n], c).then_inc(*fv.at(("f3", "r", n)))
                v.wait_ge(*fv.after(("f3", "r", n)))
                v.tensor_scalar(w, w, sm[:, 8 + n:9 + n], MAGIC, ALU.mult, ALU.add).then_inc(*fv.at(("f3", "q", n)))
                v.wait_ge(*fv.after(("f3", "q", n)))
                v.tensor_scalar(w, w, MAGIC, 1.0, ALU.subtract, ALU.min).then_inc(*fv.at(("f3", "q2", n)))
                v.wait_ge(*fv.after(("f3", "q2", n)))
                v.tensor_scalar(w, w, -1.0, None, ALU.max).then_inc(*fv.at(("f3", "w", n)))

        def f3_rms_dve(v, key, buf, width, gain, wait):
            for e in wait:
                v.wait_ge(*e)
            for t in range(T):
                if t > 0:
                    v.wait_ge(*fv.after((key, "ss", t - 1)))
                v.tensor_tensor_reduce(out=junk[:, 0:width], in0=buf[:, t, :], in1=buf[:, t, :], scale=1.0, scalar=0.0,
                                       op0=ALU.mult, op1=ALU.add, accum_out=sd[:, t:t + 1]).then_inc(*fv.at((key, "ss", t)))
            v.wait_ge(*fv.after((key, "ss", T - 1)))
            v.tensor_scalar(sd[:], sd[:], 1.0 / width, 1e-6, ALU.mult, ALU.add).then_inc(*fv.at((key, "ms")))
            v.wait_ge(*fa.after((key, "root")))
            v.reciprocal(rs[:], sd[:]).then_inc(*fv.at((key, "rs")))
            v.wait_ge(*fv.after((key, "rs")))
            for t in range(T):
                v.scalar_tensor_tensor(buf[:, t, :], buf[:, t, :], rs[:, t:t + 1], gain, ALU.mult, ALU.mult).then_inc(
                    *fv.at((key, "g") if t == T - 1 else (key, "n", t)))
            v.wait_ge(*fv.after((key, "g")))
            v.tensor_reduce(sd[:], buf, AX.X, ALU.max, apply_absolute_value=True).then_inc(*fv.at((key, "amax")))
            v.wait_ge(*fv.after((key, "amax")))
            v.tensor_scalar(sd[:], sd[:], 1e-5, None, ALU.max).then_inc(*fv.at((key, "am1")))
            v.wait_ge(*fv.after((key, "am1")))
            v.reciprocal(rs[:], sd[:]).then_inc(*fv.at((key, "am2")))
            v.tensor_scalar(mt[:, :, 0], sd[:], 1.0 / 127.0, None, ALU.mult).then_inc(*fv.at((key, "back")))
            v.wait_ge(*fv.after((key, "back")))
            v.tensor_scalar(rs[:], rs[:], 127.0, None, ALU.mult).then_inc(*fv.at((key, "am3")))
            v.wait_ge(*fv.after((key, "am3")))
            for t in range(T):
                v.tensor_scalar(buf[:, t, :], buf[:, t, :], rs[:, t:t + 1], MAGIC, ALU.mult, ALU.add).then_inc(*fv.at((key, "q1", t)))
            for t in range(T):
                v.wait_ge(*fv.after((key, "q1", t)))
                v.tensor_scalar(buf[:, t, :], buf[:, t, :], MAGIC, 127.0, ALU.subtract, ALU.min).then_inc(*fv.at((key, "q", t)))

        def f3_root_act(a, key):
            a.wait_ge(*fv.after((key, "ms")))
            a.activation(sd[:], sd[:], ACT.Sqrt).then_inc(*fa.at((key, "root")))

        def f3_dve(v):
            f3_quant_dve(v)
            norm_dve(v, 10, *turn_norm[10])
            v.wait_ge(*bias_in.after(("f3", "g")))
            f3_rms_dve(v, "f3", tok[:], D, bb[:], [tokr.after((10, t)) for t in range(T)])
            v.tensor_tensor(mm[:, :, 0], mt[:, :, 0], sm[0:Q, 4:5].to_broadcast([Q, T]), ALU.mult).then_inc(*fv.at(("f3", "back_in")))
            for t in range(T):
                v.wait_ge(*fa.after(("f3", "silu", t)))
                v.wait_ge(*fv.after(("f3", "back_in")))
                v.scalar_tensor_tensor(yy[:, t, :], bank(("f3", "h", t))[0:Q, 0:F3], mm[:, t, 0:1], gt[:, t, :], ALU.mult,
                                       ALU.mult).then_inc(*frees(("f3", "h", t), fv, ("f3", "y", t)))
            v.wait_ge(*fd.after("f3"))
            f3_rms_dve(v, "f3o", yy, F3, f3go, [fv.after(("f3", "y", T - 1))])
            v.tensor_tensor(mm[:, :, 1], mt[:, :, 0], sm[0:Q, 5:6].to_broadcast([Q, T]), ALU.mult).then_inc(*fv.at(("f3", "back_out")))
            v.wait_ge(*fv.after(("f3", "back_out")))
            for t in range(T):
                for hf in range(2):
                    y = x[:, t, hf * HD:(hf + 1) * HD]
                    v.wait_ge(*done.after(("f3", "o", t, hf)))
                    v.scalar_tensor_tensor(y, bank(("f3", "o", t, hf))[0:Q, 0:HD], mm[:, t, 1:2], y, ALU.mult,
                                           ALU.add).then_inc(*frees(("f3", "o", t, hf), fv, ("f3", "x", t, hf)))

        def f3_pool(g):
            for n in range(2):
                pool_wait(g)
                g.wait_ge(*fv.after(("f3", "sum", n)))
                g.partition_all_reduce(sm[:, 4 + n:5 + n], sm[:, 2 + n:3 + n], 128, RADD).then_inc(*pool_event(fg, ("f3", "sum", n)))

        def f3_pe(pe):
            for n, (name, wd) in enumerate((("wi", 128), ("wo", F3))):
                w = raw(("f3", name))[:, 0, 0:(D if n == 0 else K * F3)]
                for b in range(2):
                    ps = open_job(pe, ("f3", name, b))
                    pe.wait_ge(*fv.after(("f3", "w", n)))
                    for j in range(3):
                        k = 3 * b + j
                        m = pe.transpose(ps[0:wd, j * 128:(j + 1) * 128], w[:, k * wd:(k + 1) * wd], ident[:, :])
                    m.then_inc(*done.at(("f3", name, b)))
            for t in range(T):
                pe.wait_ge(*fv.after(("f3", "q", t)))
                for b in range(2):
                    ps = open_job(pe, ("turn", 10, t, b))
                    for j in range(3):
                        k = 3 * b + j
                        m = pe.transpose(ps[:, j * Q:(j + 1) * Q], tok[:, t, k * 128:(k + 1) * 128], ident[0:Q, 0:Q])
                    m.then_inc(*done.at(("turn", 10, t, b)))
            for t in range(T):
                pe.wait_ge(*fa.after(("f3", "xq", t, 1)))
                ps = open_job(pe, ("f3", "h", t))
                for k in range(K):
                    m = pe.matmul(ps[0:Q, 0:128], xq[:, k, t * Q:(t + 1) * Q], f3wi[:, k * 128:(k + 1) * 128],
                                  start=k == 0, stop=k == K - 1)
                m.then_inc(*done.at(("f3", "h", t)))
            for t in range(T):
                ps = open_job(pe, ("f3", "yT", t))
                pe.wait_ge(*fv.after(("f3o", "q", t)))
                pe.transpose(ps[0:F3, 0:Q], yy[:, t, :], ident[0:Q, 0:Q]).then_inc(*done.at(("f3", "yT", t)))
            for t in range(T):
                pe.wait_ge(*fa.after(("f3", "yq", t)))
                for hf in range(2):
                    ps = open_job(pe, ("f3", "o", t, hf))
                    pe.matmul(ps[0:Q, 0:HD], yq[:, t * Q:(t + 1) * Q], f3wo[:, hf * HD:(hf + 1) * HD], start=True,
                              stop=True).then_inc(*done.at(("f3", "o", t, hf)))

        def f3_act(a):
            a.wait_ge(*gnn_end(6, pl))
            a.wait_ge(*agv.after((6, "n1", REL - 1, 0, T - 1)))
            for n, (name, wd, dst) in enumerate((("wi", 128, f3wi), ("wo", F3, f3wo))):
                for b in range(2):
                    a.wait_ge(*done.after(("f3", name, b)))
                    a.activation(dst[:, b * HD:(b + 1) * HD], bank(("f3", name, b))[0:wd, 0:HD], ACT.Copy).then_inc(
                        *frees(("f3", name, b), fa, ("f3", name, b)))
            norm_act(a, 10)
            f3_root_act(a, "f3")
            for t in range(T):
                for b in range(2):
                    a.wait_ge(*done.after(("turn", 10, t, b)))
                    a.activation(xq[:, 3 * b:3 * b + 3, t * Q:(t + 1) * Q],
                                 bank(("turn", 10, t, b))[:, 0:3 * Q].rearrange("p (j q) -> p j q", q=Q),
                                 ACT.Copy).then_inc(*frees(("turn", 10, t, b), fa, ("f3", "xq", t, b)))
            a.wait_ge(*fv.after(("f3", "back_in")))
            a.wait_ge(*bcg.after(("R2", 6, REL - 1, 0)))
            for t in range(T):
                a.wait_ge(*done.after(("f3", "h", t)))
                a.activation(gt[:, t, :], bank(("f3", "h", t))[0:Q, F3:2 * F3], ACT.Silu, scale=mm[:, t, 0:1]).then_inc(*fa.at(("f3", "silu", t)))
            f3_root_act(a, "f3o")
            for t in range(T):
                a.wait_ge(*done.after(("f3", "yT", t)))
                a.activation(yq[:, t * Q:(t + 1) * Q], bank(("f3", "yT", t))[0:F3, 0:Q], ACT.Copy).then_inc(
                    *frees(("f3", "yT", t), fa, ("f3", "yq", t)))

        def degree_act(a):
            a.wait_ge(*cnt.after("deg"))
            a.activation(dis[:], deg[:], ACT.Sqrt).then_inc(*disa.at(0))

        stages = [
            None,
            dict(pe=lambda e: (gnn_pe(e, L[0]), gnn_pe(e, L[1])), act=lambda e: (gnn_act(e, L[0]), gnn_act(e, L[1])),
                 dve=lambda e: (gnn_dve(e, L[0]), gnn_dve(e, L[1])), pool=lambda e: (gnn_pool(e, L[0], 0), gnn_pool(e, L[1], 0)),
                 sp=lambda e: (gnn_sp(e, L[0]), gnn_sp(e, L[1])), out=lambda: [agr.after((1, "fin", d, 3)) for d in range(T)]),
            dict(pe=f0_pe, act=f0_act, dve=f0_dve, pool=f0_pool, sp=f0_sp, out=lambda: [fv.after(("f0", "x", T - 1))]),
            dict(pe=lambda e: (gnn_pe(e, L[2]), gnn_pe(e, L[3])), act=lambda e: (gnn_act(e, L[2]), gnn_act(e, L[3])),
                 dve=lambda e: (gnn_dve(e, L[2]), gnn_dve(e, L[3])), pool=lambda e: (gnn_pool(e, L[2], 3), gnn_pool(e, L[3], 3)),
                 sp=lambda e: (gnn_sp(e, L[2]), gnn_sp(e, L[3])), out=lambda: [agr.after((3, "fin", T - 1, 1))]),
            dict(pe=f1_pe, act=f1_act, dve=f1_dve, pool=f1_pool, sp=f1_sp, out=lambda: [fv.after(("f1", "x", T - 1))]),
            dict(pe=lambda e: gnn_pe(e, L[4]), act=lambda e: (degree_act(e), gnn_act(e, L[4])), dve=lambda e: gnn_dve(e, L[4]),
                 pool=lambda e: gnn_pool(e, L[4], 6), sp=lambda e: gnn_sp(e, L[4]), out=lambda: [agr.after((4, "fin", T - 1, 1))]),
            dict(pe=f2_pe, act=f2_act, dve=f2_dve, pool=f2_pool, sp=f2_sp, out=lambda: [fv.after(("f2", "x", NE - 1, T - 1, 1))]),
            dict(pe=lambda e: (gnn_pe(e, L[5]), gnn_pe(e, L[6])), act=lambda e: (gnn_act(e, L[5]), gnn_act(e, L[6])),
                 dve=lambda e: (gnn_dve(e, L[5]), gnn_dve(e, L[6])), pool=lambda e: (gnn_pool(e, L[5], 8), gnn_pool(e, L[6], 8)),
                 sp=lambda e: (gnn_sp(e, L[5]), gnn_sp(e, L[6])), out=lambda: [agr.after((6, "fin", T - 1, 1))]),
            dict(pe=f3_pe, act=f3_act, dve=f3_dve, pool=f3_pool, sp=f3_sp, out=lambda: [fv.after(("f3", "x", T - 1, 1))]),
        ][:STAGE + 1]

        def store_sp(sp, events):
            for e in events:
                sp.wait_ge(*e)
            s = sig("out_stored")
            sp.dma_start(out.rearrange("(t p) d -> p t d", p=Q), x[:]).then_inc(*s.at("out", 16))
            sp.wait_ge(*s.after("out"))

        block = ctx.enter_context(nc.Block())

        @block.tensor
        def _(pe):
            counts_pe(pe)
            for stage in stages[1:]:
                stage["pe"](pe)

        @block.vector
        def _(v):
            counts_dve(v)
            for stage in stages[1:]:
                stage["dve"](v)

        @block.scalar
        def _(a):
            for stage in stages[1:]:
                stage["act"](a)

        @block.gpsimd
        def _(g):
            consts_pool(g)
            for stage in stages[1:]:
                stage["pool"](g)

        @block.sync
        def _(sp):
            counts_sp(sp)
            params_sp(sp)
            counts_store(sp)
            for stage in stages[1:]:
                stage["sp"](sp)
            store_sp(sp, stages[-1]["out"]())


def program(make, ins):
    book = {}
    for final in (False, True):
        nc = make()
        I = {}
        for n, a in ins.items():
            I[n] = nc.dram_tensor(f"in_{n}_dram", a.shape, mybir.dt.from_np(a.dtype), kind="ExternalInput").ap()
        out = nc.dram_tensor("out_0_dram", (N, D), F32, kind="ExternalOutput").ap()
        scratch = {
            "mask": nc.dram_tensor("mask_by_type", (REL + 1, N, N), BF16, kind="Internal").ap(),
            "ct": nc.dram_tensor("counts_by_type", (REL, N, N), U16, kind="Internal").ap(),
        }
        if final:
            book["final"] = True
        build(nc, I, out, book, scratch)
    return nc


def kernel(**inputs):
    import concourse.bacc as _bacc
    from concourse.bass_utils import run_bass_kernel_spmd as _run

    arrays = {n: np.ascontiguousarray(a).reshape(np.shape(a) or (1,)) for n, a in inputs.items()}
    nc = program(lambda: _bacc.Bacc("TRN2", target_bir_lowering=False, num_devices=1), arrays)
    r = _run(nc, [{f"in_{n}_dram": a for n, a in arrays.items()}], core_ids=[0])
    return r.results[0]["out_0_dram"]
```
